# Optimizing a Trainium2 kernel written in Bass

```python
import numpy as np
import jax
import jax.numpy as jnp

def _softmax(x, axis=-1):
    return jax.nn.softmax(x, axis=axis)

def _gelu(x):
    return jax.nn.gelu(x, approximate=True)

def _silu(x):
    return jax.nn.silu(x)

def _sigmoid(x):
    return jax.nn.sigmoid(x)

def _layernorm(x, axis=-1, eps=1e-05):
    m = jnp.mean(x, axis=axis, keepdims=True)
    v = jnp.var(x, axis=axis, keepdims=True)
    return (x - m) / jnp.sqrt(v + eps)

def _scatter_add(tgt, idx, src, axis=0):
    return tgt.at[idx].add(src)

def _segment_sum(src, seg, n):
    return jax.ops.segment_sum(src, seg, n)
kernel_name = 'mk_prb_d1_jaxref_r4_d62a74'

def setup_inputs(seed: int=0):
    np.random.seed(seed)
    _w = jnp.asarray

    def _L0_attn_setup():
        import jax, jax.numpy as jnp
        import numpy as np
        B, N, D = (4, 1024, 256)
        H, F = (16, 64)
        HD = D // H
        EPS_ATTN = 1e-08
        EPS_LN = 1e-05

        def _layernorm(x, gamma, beta):
            mu = jnp.mean(x, axis=-1, keepdims=True)
            var = jnp.var(x, axis=-1, keepdims=True)
            return (x - mu) * jax.lax.rsqrt(var + EPS_LN) * gamma + beta
        key = jax.random.key(seed)
        ks = jax.random.split(key, 10)

        def kaiming(k, shape):
            fan_in = shape[1]
            return jax.random.normal(k, shape, jnp.float32) * jnp.sqrt(2.0 / fan_in)
        pm = jax.random.normal(ks[0], (H, HD, F), jnp.float32)
        return {'x': jax.random.normal(ks[1], (B, N, D), jnp.float32), 'proj': pm, 'w_qkv': kaiming(ks[2], (3 * D, D)), 'w_out': kaiming(ks[3], (D, D)), 'b_out': jnp.zeros((D,), jnp.float32), 'gamma': jnp.ones((D,), jnp.float32), 'beta': jnp.zeros((D,), jnp.float32), 'w1': kaiming(ks[4], (4 * D, D)), 'b1': jnp.zeros((4 * D,), jnp.float32), 'w2': kaiming(ks[5], (D, 4 * D)), 'b2': jnp.zeros((D,), jnp.float32)}
    _L0_attn_in = _L0_attn_setup()

    def _L0_ffn_setup():
        import jax, jax.numpy as jnp
        import numpy as np
        LN_EPS = 0.001
        EPS = 1e-05
        QB = 128.0

        def ste_round(x):
            return x + jax.lax.stop_gradient(jnp.round(x) - x)
        key = jax.random.key(seed)
        k1, k2 = jax.random.split(key)
        x = jax.random.normal(k1, (4, 2048, 256), dtype=jnp.float32)
        weight = jax.random.normal(k2, (256, 256), dtype=jnp.float32) * 0.02
        ln_gamma = jnp.ones((256,), dtype=jnp.float32)
        ln_beta = jnp.zeros((256,), dtype=jnp.float32)
        return {'x': x, 'weight': weight, 'ln_gamma': ln_gamma, 'ln_beta': ln_beta}
    _L0_ffn_in = _L0_ffn_setup()
    _d = {'L0_attn_x': _L0_attn_in['x'], 'L0_attn_proj': _L0_attn_in['proj'], 'L0_attn_w_qkv': _L0_attn_in['w_qkv'], 'L0_attn_w_out': _L0_attn_in['w_out'], 'L0_attn_b_out': _L0_attn_in['b_out'], 'L0_attn_gamma': _L0_attn_in['gamma'], 'L0_attn_beta': _L0_attn_in['beta'], 'L0_attn_w1': _L0_attn_in['w1'], 'L0_attn_b1': _L0_attn_in['b1'], 'L0_attn_w2': _L0_attn_in['w2'], 'L0_attn_b2': _L0_attn_in['b2'], 'L0_ffn_weight': _L0_ffn_in['weight'], 'L0_ffn_ln_gamma': _L0_ffn_in['ln_gamma'], 'L0_ffn_ln_beta': _L0_ffn_in['ln_beta']}
    _x0 = _d['L0_attn_x']
    _d['L0_attn_x'] = jax.random.normal(jax.random.fold_in(jax.random.key(seed), 1), (8, 2048, 256), dtype=_x0.dtype)
    del _x0
    return _d

def reference(L0_attn_x, L0_attn_proj, L0_attn_w_qkv, L0_attn_w_out, L0_attn_b_out, L0_attn_gamma, L0_attn_beta, L0_attn_w1, L0_attn_b1, L0_attn_w2, L0_attn_b2, L0_ffn_weight, L0_ffn_ln_gamma, L0_ffn_ln_beta):

    def _L0_attn_ref(x, proj, w_qkv, w_out, b_out, gamma, beta, w1, b1, w2, b2):
        import jax, jax.numpy as jnp
        import numpy as np
        B, N, D = (4, 1024, 256)
        H, F = (16, 64)
        HD = D // H
        EPS_ATTN = 1e-08
        EPS_LN = 1e-05

        def _layernorm(x, gamma, beta):
            mu = jnp.mean(x, axis=-1, keepdims=True)
            var = jnp.var(x, axis=-1, keepdims=True)
            return (x - mu) * jax.lax.rsqrt(var + EPS_LN) * gamma + beta
        residual = x
        b, n, d = x.shape
        qkv = x @ w_qkv.T
        q, k, v = jnp.split(qkv, 3, axis=-1)

        def to_heads(t):
            return t.reshape(b, n, H, HD).transpose(0, 2, 1, 3)
        q, k, v = (to_heads(q), to_heads(k), to_heads(v))
        q_f = jax.nn.elu(jnp.einsum('bhnd,hdf->bhnf', q, proj)) + 1.0
        k_f = jax.nn.elu(jnp.einsum('bhnd,hdf->bhnf', k, proj)) + 1.0
        kv = jnp.einsum('bhnf,bhnd->bhfd', k_f, v)
        attn = jnp.einsum('bhnf,bhfd->bhnd', q_f, kv)
        k_sum = jnp.sum(k_f, axis=2)
        z = 1.0 / (jnp.einsum('bhnf,bhf->bhn', q_f, k_sum) + EPS_ATTN)
        attn = attn * z[..., None]
        attn = attn.transpose(0, 2, 1, 3).reshape(b, n, d)
        x = residual + attn @ w_out.T + b_out
        x = _layernorm(x, gamma, beta)
        h = jax.nn.gelu(x @ w1.T + b1, approximate=False)
        x = x + h @ w2.T + b2
        x = _layernorm(x, gamma, beta)
        return x

    def _L0_ffn_ref(x, weight, ln_gamma, ln_beta):
        import jax, jax.numpy as jnp
        import numpy as np
        LN_EPS = 0.001
        EPS = 1e-05
        QB = 128.0

        def ste_round(x):
            return x + jax.lax.stop_gradient(jnp.round(x) - x)
        mu = jnp.mean(x, axis=-1, keepdims=True)
        var = jnp.var(x, axis=-1, keepdims=True)
        xn = (x - mu) * jax.lax.rsqrt(var + LN_EPS) * ln_gamma + ln_beta
        beta = jnp.mean(jnp.abs(weight))
        w_q = jnp.clip(ste_round(weight / (beta + EPS)), -1.0, 1.0)
        gamma = jnp.max(jnp.abs(xn))
        xq = jnp.clip(xn * QB / gamma, -QB + EPS, QB - EPS)
        y = jnp.einsum('bsd,du->bsu', xq, w_q)
        return y * (gamma * beta / QB)
    x = L0_attn_x
    xn = _layernorm(x, axis=-1)
    x = x + _L0_attn_ref(xn, L0_attn_proj, L0_attn_w_qkv, L0_attn_w_out, L0_attn_b_out, L0_attn_gamma, L0_attn_beta, L0_attn_w1, L0_attn_b1, L0_attn_w2, L0_attn_b2) + _L0_ffn_ref(xn, L0_ffn_weight, L0_ffn_ln_gamma, L0_ffn_ln_beta)
    return x

_drawn_inputs = setup_inputs


def setup_inputs(seed=0):
    import zlib

    import numpy as np

    out = dict(_drawn_inputs(seed))
    spreads = {'L0_attn_b_out': (0.0, 0.1),
     'L0_attn_gamma': (1.0, 0.2),
     'L0_attn_beta': (0.0, 0.1),
     'L0_attn_b1': (0.0, 0.1),
     'L0_attn_b2': (0.0, 0.1),
     'L0_ffn_ln_gamma': (1.0, 0.6),
     'L0_ffn_ln_beta': (0.0, 0.73)}
    factors = {'L0_attn_proj': 8.607}
    for name, (base, spread) in spreads.items():
        noise = np.random.default_rng([zlib.crc32(name.encode()), seed]).standard_normal(out[name].shape)
        drawn = base * np.exp(spread * noise) if base else spread * noise
        out[name] = jnp.asarray(drawn.astype(out[name].dtype))
    for name, factor in factors.items():
        out[name] = (out[name] * factor).astype(out[name].dtype)
    return out
```

```python
from contextlib import ExitStack

import concourse.bass as bass
from concourse import mybir

F32 = mybir.dt.float32
F32R = mybir.dt.float32r
ALU = mybir.AluOpType
ACT = mybir.ActivationFunctionType
AX_X = mybir.AxisListType.X

P = 128
B, N, D = 8, 2048, 256
H, HD, F = 16, 16, 64
FF = 4 * D
TILES = 4
GT = TILES * P
GPB = N // GT
GROUPS = B * GPB
KD = D // P
HC = H * F // P
FC = FF // P
VW = HD + 1
CW = 2 * VW
KVW = HC * CW
PAIR = 2 * 512

EPS_LN = 1e-5
EPS_ATTN = 1e-8
EPS_FFN_LN = 1e-3
EPS_FFN = 1e-5
QB = 128.0
CLIP = QB - EPS_FFN
KV_SCALE = 1.0 / N


def nth(b, u, j=1, per=1):
    return b * (GPB * per) + (per * u + j)


def exists(b, u):
    return not isinstance(b, int) or 0 <= GPB * b + u < GROUPS


def dma_nth(b, u):
    return b * (16 * GPB // 2) + 16 * ((u - u % 2) // 2 + 1)


def over_groups(eng, step):
    for u in range(-2, GPB):
        step(0, u)
    with eng.Fori(1, B - 1) as b:
        for u in range(GPB):
            step(b, u)
    for u in range(GPB + 1):
        step(B - 1, u)


def linear_attention_block(nc, x, proj, w_qkv, w_out, b_out, gamma, beta, w1, b1, w2, b2,
                           ffn_weight, ln_gamma, ln_beta, out):
    x_rows = x.rearrange("b n d -> (b n) d").rearrange("(g p t) d -> g p t d", p=P, t=TILES)
    out_rows = out.rearrange("b n d -> (b n) d").rearrange("(g p t) d -> g p t d", p=P, t=TILES)

    with ExitStack() as ctx:
        def sb(name, shape, dt=F32):
            return ctx.enter_context(nc.sbuf_tensor(name, shape, dt))

        def sem(name):
            return ctx.enter_context(nc.semaphore(name))

        ps = ctx.enter_context(nc.psum_tensor("ps", [P, 8, 512], F32))

        def pair(s):
            return ps[:, 2 * s:2 * s + 2, :]

        def pair_flat(s):
            return pair(s).rearrange("p a b -> p (a b)")

        ident = sb("ident", [P, P])
        ones = sb("ones", [P, P])
        minus_half = sb("minus_half", [P, 8])
        kv_mask = sb("kv_mask", [P, KVW])

        def split(name, shape):
            return sb(name + "_hi", shape, F32R), sb(name + "_lo", shape, F32R)

        wq, wk, wv = (split(n, [P, KD, D]) for n in ("wq", "wk", "wv"))
        wo = split("wo", [P, KD, D])
        w1s = split("w1s", [P, KD, FF])
        w2s = split("w2s", [P, FC, D])
        projs = split("projs", [P, KD, 8 * F])
        ternary = sb("ternary", [P, KD, D], F32R)
        gamma_row, beta_row, bout_row, b2_row = (sb(n, [P, D]) for n in ("gamma_row", "beta_row", "bout_row", "b2_row"))
        gamma_col, beta_col, lng_col, lnb_col = (sb(n, [P, KD]) for n in ("gamma_col", "beta_col", "lng_col", "lnb_col"))
        b1_col = sb("b1_col", [P, FC])
        small = sb("small", [P, 32])
        w_mean, w_half, w_minus_half, gmax, qscale, y_scale, colsum = (small[:, i:i + 1] for i in range(7))
        gz, bz = small[:, 8:10], small[:, 10:12]
        zext, zabs, zpart = small[:, 12:16], small[:, 16:20], small[:, 20:21]

        xin = sb("xin", [P, 2, TILES, D])
        z = sb("z", [P, TILES, D])
        xnT = split("xnT", [P, KD, GT])
        feat = sb("feat", [P, HC, 512])
        hf = sb("hf", [P, 2, TILES, KVW])
        hid = split("hid", [P, FC, GT])
        xres = sb("xres", [P, 2, TILES, D])
        stats = sb("stats", [P, GROUPS * 12])
        stat = sb("stat", [P, 2, 12])
        kv_all = sb("kv_all", [P, B * KVW])
        kv_cur = sb("kv_cur", [P, KVW])
        qT = split("qT", [P, KD, GT])
        attn = sb("attn", [P, TILES, D])
        tT = split("tT", [P, KD, GT])
        n1 = sb("n1", [P, TILES, D])
        res1 = sb("res1", [P, TILES, D])
        res2 = sb("res2", [P, TILES, D])
        x2 = sb("x2", [P, TILES, D])
        zq = attn.rearrange("p t d -> p (t d)").rearrange("p (k t) -> p k t", k=KD)
        zs = split("zs", [P, KD, GT])
        bn = sb("bn", [P, TILES, 6])
        mv = sb("mv", [P, TILES, 2])
        pw = sb("pw", [P, 8])
        inv = sb("inv", [P, TILES])
        mv1, mv2 = sb("mv1", [P, TILES, 2]), sb("mv2", [P, TILES, 2])
        bn1, bn2 = sb("bn1", [P, TILES, 6]), sb("bn2", [P, TILES, 6])
        ve1, ve2 = sb("ve1", [P, TILES]), sb("ve2", [P, TILES])
        rs1, rs2 = sb("rs1", [P, TILES]), sb("rs2", [P, TILES])
        rden = sb("rden", [P, TILES, H])

        keys = tuple(part[:, 0:2 * KD, :].rearrange("p (k c) t -> p k c t", k=2) for part in hid)
        key_feat = feat.rearrange("p (n a) c -> p n (a c)", a=2)
        vals = hf
        hidden = hf.rearrange("p k t c -> p k (t c)")[:, :, 0:PAIR]
        zmax, zmin = xres[:, 0], xres[:, 1]
        raw_w1 = feat[:, 0:4, :].rearrange("p a c -> p (a c)").rearrange("p (r d) -> p r d", d=D)
        raw_w2 = feat[:, 4:8, :].rearrange("p a c -> p (a c)").rearrange("p (r f) -> p r f", f=FF)
        raw_qkv = xin.rearrange("p k t d -> p (k t) d")[:, 0:6, :]
        raw_out = xin.rearrange("p k t d -> p (k t) d")[:, 6:8, :]
        raw_proj = attn.rearrange("p t d -> p (t d)").rearrange("p (k c) -> p k c", k=KD)
        raw_ffn = n1[:, 0:2, :]
        w1T = xres.rearrange("p k t d -> p k (t d)")
        tern_a, tern_b = res1.rearrange("p t d -> p (t d)")[:, 0:KD * D], res2.rearrange("p t d -> p (t d)")[:, 0:KD * D]

        consts_set, proj_zero, mask_zero, mask_ready = sem("consts_set"), sem("proj_zero"), sem("mask_zero"), sem("mask_ready")
        ld_qkv, ld_w1, ld_w2, ld_ffn, ld_proj, ld_cols, ld_rows = (
            sem(n) for n in ("ld_qkv", "ld_w1", "ld_w2", "ld_ffn", "ld_proj", "ld_cols", "ld_rows"))
        wT_mm, wT_hi, wT_lo = sem("wT_mm"), sem("wT_hi"), sem("wT_lo")
        w1_plain, w1_scaled, b1_mm, b1_done = sem("w1_plain"), sem("w1_scaled"), sem("b1_mm"), sem("b1_done")
        w_abs, w_sum, w_chain, tern_done = sem("w_abs"), sem("w_sum"), sem("w_chain"), sem("tern_done")
        proj_hi, proj_lo, raw_used = sem("proj_hi"), sem("proj_lo"), sem("raw_used")
        vals_ones, zinit = sem("vals_ones"), sem("zinit")

        x_loaded = [sem("x_loaded0"), sem("x_loaded1")]
        bn_done, mv_done, ve_done, inv_done, ratio_done, pw_ready = (
            sem(n) for n in ("bn_done", "mv_done", "ve_done", "inv_done", "ratio_done", "pw_ready"))
        std_ready, xn_ready, z_ready, z_used, stat_saved = (
            sem(n) for n in ("std_ready", "xn_ready", "z_ready", "z_used", "stat_saved"))
        xnT_mm, xnT_hi, xnT_lo = sem("xnT_mm"), sem("xnT_hi"), sem("xnT_lo")
        kT_mm, kT_hi, kT_lo = sem("kT_mm"), sem("kT_hi"), sem("kT_lo")
        v_mm, v_ready = sem("v_mm"), sem("v_ready")
        kf_mm, kf_neg, kf_exp, kf_ready = sem("kf_mm"), sem("kf_neg"), sem("kf_exp"), sem("kf_ready")
        kv_mm, kv_saved = sem("kv_mm"), sem("kv_saved")

        pool_held, dve_held = sem("pool_held"), sem("dve_held")
        zmT_in, scales_y = sem("zmT_in"), sem("scales_y")
        zm_part, zm_done, zmT_mm, zext_done, g_chain, zpart_mm, g_one, g_all, scales_ready = (
            sem(n) for n in ("zm_part", "zm_done", "zmT_mm", "zext_done", "g_chain", "zpart_mm", "g_one", "g_all", "scales_ready"))

        x2_loaded = [sem("x2_loaded0"), sem("x2_loaded1")]
        r_loaded = [sem("r_loaded0"), sem("r_loaded1")]
        stored = [sem("stored0"), sem("stored1")]
        stat_got, xnb_ready, zb_ready, res1_ready = (sem(n) for n in ("stat_got", "xnb_ready", "zb_ready", "res1_ready"))
        kv_ready = sem("kv_ready")
        xT_mm, xT_hi, xT_lo = sem("xT_mm"), sem("xT_hi"), sem("xT_lo")
        qT_mm, qT_hi, qT_lo = sem("qT_mm"), sem("qT_hi"), sem("qT_lo")
        qf_mm, qf_neg, qf_exp, qf_ready = sem("qf_mm"), sem("qf_neg"), sem("qf_exp"), sem("qf_ready")
        at_mm, den_done, rden_done, at_ready = sem("at_mm"), sem("den_done"), sem("rden_done"), sem("at_ready")
        aT_mm, aT_hi, aT_lo = sem("aT_mm"), sem("aT_hi"), sem("aT_lo")
        wo_mm, x1_sum, bn1_done, mv1_done, ve1_ready, rs1_ready, n1_ready = (
            sem(n) for n in ("wo_mm", "x1_sum", "bn1_done", "mv1_done", "ve1_ready", "rs1_ready", "n1_ready"))
        res2_part, res2_ready = sem("res2_part"), sem("res2_ready")
        nT_mm, nT_hi, nT_lo = sem("nT_mm"), sem("nT_hi"), sem("nT_lo")
        w1_mm, gelu_done, h_hi, h_lo, w2_mm = (sem(n) for n in ("w1_mm", "gelu_done", "h_hi", "h_lo", "w2_mm"))
        x2_sum, bn2_done, mv2_done, ve2_ready, rs2_ready, x2_scaled, out_ready = (
            sem(n) for n in ("x2_sum", "bn2_done", "mv2_done", "ve2_ready", "rs2_ready", "x2_scaled", "out_ready"))
        zT_mm, zq_affine, zq_clipped, zs_hi, zs_lo, y_mm, xb_ready, acc_ready = (
            sem(n) for n in ("zT_mm", "zq_affine", "zq_clipped", "zs_hi", "zs_lo", "y_mm", "xb_ready", "acc_ready"))

        def three_passes(pe, dst, weights, moving, chunks, first=True, last=True):
            steps = [(c, i, j) for c in chunks for i, j in ((0, 0), (0, 1), (1, 0))]
            for n, (c, i, j) in enumerate(steps):
                mm = pe.matmul(dst, weights(c)[i], moving(c)[j], start=first and n == 0,
                               stop=last and n == len(steps) - 1)
            return mm

        def columns(parts, cols):
            return lambda c: tuple(p[:, c, cols] for p in parts)

        def tile_cols(t):
            return slice(t * P, (t + 1) * P)

        def group(b, u):
            return b * GPB + u

        def stat_cols(b, u):
            return stats[:, bass.ds(group(b, u) * 12, 12)]

        def kv_cols(b):
            return kv_all[:, bass.ds(b * KVW, KVW)]

        WEIGHT_SLOTS = (0, 1, 2, 3, 0, 1)

        def weight_blocks(n):
            if n < 2:
                raws = ((raw_qkv, 0), (raw_qkv, 2)) if n == 0 else ((raw_qkv, 4), (raw_out, 0))
                return [((2 * i + c) * D + r * P, raw[:, base + r, tile_cols(c)])
                        for i, (raw, base) in enumerate(raws) for c in range(KD) for r in range(2)]
            if n < 4:
                return [(r * P, raw_w1[:, r, tile_cols(n - 2)]) for r in range(FC)]
            return [(j * D + r * P, raw_w2[:, r, tile_cols(4 * (n - 4) + j)]) for j in range(4) for r in range(2)]

        def weight_parts(n, part):
            if n < 2:
                return [(w[part][:].rearrange("p k d -> p (k d)"), ps[:, 2 * n + i, :])
                        for i, w in enumerate(((wq, wk), (wv, wo))[n])]
            return [(w2s[part][:, 4 * (n - 4):4 * (n - 3), :].rearrange("p k d -> p (k d)"), pair_flat(WEIGHT_SLOTS[n]))]

        block = ctx.enter_context(nc.Block())

        @block.sync
        def _(sp):
            sp.dma_start(raw_qkv, w_qkv.rearrange("(r p) d -> p r d", p=P)).then_inc(ld_qkv, 16)
            sp.dma_start(raw_out, w_out.rearrange("(r p) d -> p r d", p=P)).then_inc(ld_qkv, 16)
            sp.dma_start(raw_w1, w1.rearrange("(r p) d -> p r d", p=P)).then_inc(ld_w1, 16)
            sp.dma_start(raw_w2, w2.rearrange("(r p) f -> p r f", p=P)).then_inc(ld_w2, 16)
            sp.dma_start(raw_ffn, ffn_weight.rearrange("(k p) u -> p k u", p=P)).then_inc(ld_ffn, 16)
            for dst, src in ((gamma_col, gamma), (beta_col, beta), (lng_col, ln_gamma), (lnb_col, ln_beta), (b1_col, b1)):
                sp.dma_start(dst[:], src.rearrange("(k p) -> p k", p=P), allow_slow_non_contiguous=True).then_inc(ld_cols, 16)
            for dst, src in ((gamma_row, gamma), (beta_row, beta), (bout_row, b_out), (b2_row, b2)):
                sp.dma_start(dst[:], src.partition_broadcast(P)).then_inc(ld_rows, 16)
            sp.wait_ge(proj_zero, 1)
            for h in range(H):
                r = h % 8
                sp.dma_start(raw_proj[r * HD:(r + 1) * HD, h // 8, r * F:(r + 1) * F], proj[h]).then_inc(ld_proj, 16)
            sp.wait_ge(wT_mm, 2)

            def load_a(b, u):
                if not exists(b, u + 2):
                    return
                if exists(b, u):
                    sp.wait_ge(xnT_mm, nth(b, u))
                    sp.wait_ge(z_ready, nth(b, u))
                k = u % 2
                sp.dma_start(xin[:, k], x_rows[group(b, u + 2)]).then_inc(x_loaded[k], 16)

            over_groups(sp, load_a)
            sp.wait_ge(xnT_mm, GROUPS)
            sp.wait_ge(z_ready, GROUPS)

            def move_b(b, u):
                k = u % 2
                if exists(b, u + 2):
                    if exists(b, u):
                        sp.wait_ge(xT_mm, nth(b, u))
                        sp.wait_ge(zb_ready, nth(b, u))
                    sp.dma_start(xin[:, k], x_rows[group(b, u + 2)]).then_inc(x2_loaded[k], 16)
                if exists(b, u - 1):
                    sp.wait_ge(out_ready, nth(b, u - 1))
                    sp.dma_start(out_rows[group(b, u - 1)], xres[:, 1 - k]).then_inc(stored[1 - k], 16)
                if exists(b, u + 1):
                    if exists(b, u - 1):
                        sp.wait_ge(stored[1 - k], dma_nth(b, u - 1))
                    else:
                        sp.wait_ge(zm_done, 1)
                    sp.dma_start(xres[:, 1 - k], x_rows[group(b, u + 1)]).then_inc(r_loaded[1 - k], 16)

            over_groups(sp, move_b)
            for s in stored:
                sp.wait_ge(s, 16 * GROUPS // 2)

        @block.gpsimd
        def _(pool):
            def hold():
                pool.sem_inc(pool_held, 1)

            pool.memset(ones[:], 1.0).then_inc(consts_set, 1)
            pool.memset(minus_half[:], -0.5).then_inc(consts_set, 1)
            pool.memset(ident[:], 0.0).then_inc(consts_set, 1)
            pool.wait_ge(consts_set, 3)
            pool.affine_select(out=ident[:], in_=ident[:], compare_op=ALU.not_equal, fill=1.0, base=0,
                               pattern=[[-1, P]], channel_multiplier=1).then_inc(consts_set, 1)

            def norm_a(b, u):
                if not exists(b, u + 2):
                    return
                k = u % 2
                pool.wait_ge(pw_ready, nth(b, u + 2))
                pool.tensor_tensor(stat[:, k, 0:8], pw[:], minus_half[:], ALU.pow).then_inc(std_ready, 1)
                pool.wait_ge(std_ready, nth(b, u + 2))
                hold()
                for t in range(TILES):
                    last = pool.tensor_scalar(xin[:, k, t, :], xin[:, k, t, :], stat[:, k, 8 + t:9 + t],
                                              stat[:, k, t:t + 1], ALU.add, ALU.mult)
                last.then_inc(xn_ready, 1)
                pool.wait_ge(xn_ready, nth(b, u + 2))
                if exists(b, u + 1):
                    pool.wait_ge(z_used, nth(b, u + 1))
                hold()
                for t in range(TILES):
                    last = pool.tensor_scalar(z[:, t, :], xin[:, k, t, :], stat[:, k, 4 + t:5 + t], 1.0,
                                              ALU.mult, ALU.mult)
                last.then_inc(z_ready, 1)

            over_groups(pool, norm_a)
            pool.wait_ge(z_used, GROUPS)
            pool.wait_ge(xnT_mm, GROUPS)

            def step_b(b, u):
                k = u % 2
                flat = lambda a: a.rearrange("p t d -> p (t d)")
                if exists(b, u - 1):
                    pool.wait_ge(ve2_ready, nth(b, u - 1))
                    pool.tensor_tensor(rs2[:], ve2[:], minus_half[:, 0:TILES], ALU.pow).then_inc(rs2_ready, 1)
                if exists(b, u):
                    pool.wait_ge(n1_ready, nth(b, u))
                    if exists(b, u - 1):
                        pool.wait_ge(x2_sum, nth(b, u - 1))
                    pool.tensor_tensor(res2[:], n1[:], gamma_row[:].unsqueeze(1).broadcast_to([P, TILES, D]),
                                       ALU.mult).then_inc(res2_part, 1)
                    pool.wait_ge(res2_part, nth(b, u))
                    pool.tensor_tensor(res2[:], res2[:], b2_row[:].unsqueeze(1).broadcast_to([P, TILES, D]),
                                       ALU.add).then_inc(res2_ready, 1)
                    for p in range(FC // 2):
                        pool.wait_ge(h_hi, nth(b, u, p + 1, 4))
                        pool.tensor_tensor(hid[1][:, 2 * p:2 * p + 2, :].rearrange("p a c -> p (a c)"),
                                           hidden[:, p % 2], hid[0][:, 2 * p:2 * p + 2, :].rearrange("p a c -> p (a c)").bitcast(F32),
                                           ALU.subtract).then_inc(h_lo, 1)
                    pool.wait_ge(r_loaded[k], dma_nth(b, u))
                    pool.tensor_tensor(xres[:, k], xres[:, k], beta_row[:].unsqueeze(1).broadcast_to([P, TILES, D]),
                                       ALU.add).then_inc(xb_ready, 1)
                if exists(b, u + 2):
                    pool.wait_ge(x2_loaded[k], dma_nth(b, u + 2))
                    pool.wait_ge(stat_got, nth(b, u + 2))
                    hold()
                    for t in range(TILES):
                        last = pool.tensor_scalar(xin[:, k, t, :], xin[:, k, t, :], stat[:, k, 8 + t:9 + t],
                                                  stat[:, k, t:t + 1], ALU.add, ALU.mult)
                    last.then_inc(xnb_ready, 1)
                if exists(b, u + 1):
                    pool.wait_ge(zs_hi, nth(b, u + 1))
                    if exists(b, u):
                        pool.wait_ge(y_mm, nth(b, u))
                    pool.tensor_tensor(zs[1][:], zq, zs[0][:].bitcast(F32), ALU.subtract).then_inc(zs_lo, 1)
                    pool.wait_ge(ve1_ready, nth(b, u + 1))
                    pool.tensor_tensor(rs1[:], ve1[:], minus_half[:, 0:TILES], ALU.pow).then_inc(rs1_ready, 1)
                if exists(b, u + 2):
                    pool.wait_ge(xnb_ready, nth(b, u + 2))
                    if exists(b, u + 1):
                        pool.wait_ge(x1_sum, nth(b, u + 1))
                    pool.tensor_tensor(res1[:], xin[:, k], bout_row[:].unsqueeze(1).broadcast_to([P, TILES, D]),
                                       ALU.add).then_inc(res1_ready, 1)
                    if exists(b, u + 1):
                        pool.wait_ge(zT_mm, nth(b, u + 1))
                    hold()
                    for t in range(TILES):
                        last = pool.tensor_scalar(z[:, t, :], xin[:, k, t, :], stat[:, k, 4 + t:5 + t], 1.0,
                                                  ALU.mult, ALU.mult)
                    last.then_inc(zb_ready, 1)

            over_groups(pool, step_b)

        @block.scalar
        def _(act):
            for n, s in enumerate(WEIGHT_SLOTS):
                act.wait_ge(wT_mm, n + 1)
                if n in (2, 3):
                    act.copy(w1T[:, n - 2, :], pair_flat(s)).then_inc(w1_plain, 1)
                    continue
                for hi, src in weight_parts(n, 0):
                    last = act.copy(hi, src)
                last.then_inc(wT_hi, 1)
            act.wait_ge(w1_scaled, 1)
            act.copy(w1s[0][:], w1T).then_inc(wT_hi, 1)
            act.wait_ge(ld_proj, 16 * H)
            act.copy(projs[0][:], raw_proj).then_inc(proj_hi, 1)
            act.wait_ge(ld_ffn, 16)
            act.activation(tern_a, raw_ffn.rearrange("p k u -> p (k u)"), ACT.Abs, accum_out=colsum).then_inc(w_abs, 1)

            def step_a(b, u):
                for t in range(TILES):
                    if exists(b, u):
                        act.wait_ge(kf_mm, nth(b, u, t + 1, 4))
                        if exists(b, u - 1):
                            act.wait_ge(kv_mm, nth(b, u - 1, t + 1, 4))
                        s = 1 + t % 2
                        act.activation(key_feat[:, t, :], pair_flat(s), ACT.Relu, scale=-1.0).then_inc(kf_neg, 1)
                        act.wait_ge(kf_neg, nth(b, u, t + 1, 4))
                        act.activation(key_feat[:, t, :], key_feat[:, t, :], ACT.Exp, scale=-1.0).then_inc(kf_exp, 1)
                    if not exists(b, u + 1):
                        continue
                    if t == 0:
                        act.wait_ge(xnT_mm, nth(b, u + 1))
                        if exists(b, u):
                            act.wait_ge(v_mm, nth(b, u))
                        act.copy(xnT[0][:], pair(0)).then_inc(xnT_hi, 1)
                    if t == 1:
                        act.wait_ge(kT_mm, nth(b, u + 1))
                        if exists(b, u - 1):
                            act.wait_ge(kf_mm, nth(b, u - 1, 4, 4))
                        act.copy(keys[0][:, (u + 1) % 2], pair(0)).then_inc(kT_hi, 1)
                    if t == 2:
                        act.wait_ge(v_mm, nth(b, u + 1))
                        act.wait_ge(vals_ones, 1)
                        if exists(b, u - 1):
                            act.wait_ge(kv_mm, nth(b, u - 1, 4, 4))
                        for a in range(2):
                            last = act.copy(
                                vals[:, (u + 1) % 2, 2 * a:2 * a + 2, :].rearrange("p t (h e) -> p t h e", e=VW)[:, :, :, 0:HD],
                                ps[:, a, :].rearrange("p (t h e) -> p t h e", t=2, e=HD))
                        last.then_inc(v_ready, 1)

            over_groups(act, step_a)

            def step_b(b, u):
                if exists(b, u):
                    act.wait_ge(nT_mm, nth(b, u))
                    act.wait_ge(wo_mm, nth(b, u))
                    act.copy(tT[0][:], pair(0)).then_inc(nT_hi, 1)
                    for p in range(FC // 2):
                        act.wait_ge(w1_mm, nth(b, u, p + 1, 4))
                        if p >= 2:
                            act.wait_ge(h_lo, nth(b, u, p - 1, 4))
                        elif exists(b, u - 1):
                            act.wait_ge(h_lo, nth(b, u - 1, p + 3, 4))
                        s = (p + 1) % 2
                        for a in range(2):
                            c = 2 * p + a
                            last = act.activation(hidden[:, p % 2, a * 512:(a + 1) * 512], ps[:, 2 * s + a, :],
                                                  ACT.Gelu, bias=b1_col[:, c:c + 1])
                        last.then_inc(gelu_done, 1)
                if exists(b, u + 1):
                    for p in range(HC // 2):
                        act.wait_ge(qf_mm, nth(b, u + 1, p + 1, 4))
                        if exists(b, u):
                            act.wait_ge(at_mm, nth(b, u, 2, 2))
                        q = feat[:, 2 * p:2 * p + 2, :]
                        act.activation(q, pair(2 + p % 2), ACT.Relu, scale=-1.0).then_inc(qf_neg, 1)
                        act.wait_ge(qf_neg, nth(b, u + 1, p + 1, 4))
                        act.activation(q, q, ACT.Exp, scale=-1.0).then_inc(qf_exp, 1)
                    act.wait_ge(aT_mm, nth(b, u + 1))
                    if exists(b, u):
                        act.wait_ge(w1_mm, nth(b, u, 4, 4))
                    act.copy(tT[0][:], pair(2)).then_inc(aT_hi, 1)
                    act.wait_ge(zT_mm, nth(b, u + 1))
                    act.wait_ge(scales_ready, 1)
                    if exists(b, u):
                        act.wait_ge(zs_lo, nth(b, u))
                    for c in range(KD):
                        last = act.activation(zq[:, c, :], ps[:, c, :], ACT.Identity, bias=bz[:, c:c + 1], scale=gz[:, c:c + 1])
                    last.then_inc(zq_affine, 1)
                if exists(b, u + 2):
                    act.wait_ge(xT_mm, nth(b, u + 2))
                    if exists(b, u + 1):
                        act.wait_ge(qT_mm, nth(b, u + 1))
                    act.copy(xnT[0][:], pair(2)).then_inc(xT_hi, 1)
                if exists(b, u + 1):
                    act.wait_ge(zq_clipped, nth(b, u + 1))
                    if exists(b, u):
                        act.wait_ge(y_mm, nth(b, u))
                    act.copy(zs[0][:], zq).then_inc(zs_hi, 1)
                if exists(b, u + 2):
                    act.wait_ge(qT_mm, nth(b, u + 2))
                    if exists(b, u + 1):
                        act.wait_ge(qf_mm, nth(b, u + 1, 4, 4))
                    act.copy(qT[0][:], pair(3)).then_inc(qT_hi, 1)

            over_groups(act, step_b)

        @block.vector
        def _(dve):
            def hold():
                dve.sem_inc(dve_held, 1)

            dve.memset(raw_proj, 0.0).then_inc(proj_zero, 1)
            dve.memset(kv_mask[:], 0.0).then_inc(mask_zero, 1)
            dve.wait_ge(mask_zero, 1)
            mask_c = kv_mask[:].rearrange("p (c w) -> p c w", w=CW)
            dve.memset(mask_c[0:F, :, 0:VW], KV_SCALE).then_inc(mask_ready, 1)
            dve.memset(mask_c[F:P, :, VW:CW], KV_SCALE).then_inc(mask_ready, 1)
            dve.memset(vals[:], 1.0).then_inc(vals_ones, 1)

            done = 0
            for n, s in enumerate(WEIGHT_SLOTS):
                if n in (2, 3):
                    continue
                done += 1
                dve.wait_ge(wT_hi, done)
                for (lo, src), (hi, _) in zip(weight_parts(n, 1), weight_parts(n, 0)):
                    last = dve.tensor_tensor(lo, src, hi.bitcast(F32), ALU.subtract)
                last.then_inc(wT_lo, 1)
            dve.wait_ge(b1_mm, 1)
            dve.wait_ge(ld_cols, 16 * 5)
            dve.tensor_tensor(b1_col[:], ps[:, 4, 0:FC], b1_col[:], ALU.add).then_inc(b1_done, 1)
            for c in range(KD):
                last = dve.tensor_scalar(w1T[:, c, :], w1T[:, c, :], gamma_col[:, c:c + 1], None, ALU.mult)
            last.then_inc(w1_scaled, 1)
            dve.wait_ge(wT_hi, done + 1)
            dve.tensor_tensor(w1s[1][:], w1T, w1s[0][:].bitcast(F32), ALU.subtract).then_inc(wT_lo, 1)
            dve.wait_ge(proj_hi, 1)
            dve.tensor_tensor(projs[1][:], raw_proj, projs[0][:].bitcast(F32), ALU.subtract).then_inc(proj_lo, 1)
            dve.wait_ge(ld_rows, 16 * 4)
            dve.tensor_tensor(b2_row[:], b2_row[:], beta_row[:], ALU.add).then_inc(w_chain, 1)
            dve.wait_ge(w_sum, 1)
            dve.tensor_scalar(w_mean, ps[:, 5, 0:1], 1.0 / (D * D), None, ALU.mult).then_inc(w_chain, 1)
            dve.wait_ge(w_chain, 2)
            dve.tensor_scalar(w_half, w_mean, EPS_FFN, 0.5, ALU.add, ALU.mult).then_inc(w_chain, 1)
            dve.tensor_scalar(y_scale, w_mean, 1.0 / QB, None, ALU.mult).then_inc(w_chain, 1)
            dve.wait_ge(w_chain, 3)
            dve.tensor_scalar(w_minus_half, w_half, -1.0, None, ALU.mult).then_inc(w_chain, 1)
            flat_ffn = raw_ffn.rearrange("p k u -> p (k u)")
            dve.tensor_scalar(tern_a, flat_ffn, w_half, None, ALU.is_gt).then_inc(w_chain, 1)
            dve.wait_ge(w_chain, 6)
            dve.tensor_scalar(tern_b, flat_ffn, w_minus_half, None, ALU.is_lt).then_inc(w_chain, 1)
            dve.wait_ge(w_chain, 7)
            dve.tensor_tensor(ternary[:].rearrange("p k u -> p (k u)"), tern_a, tern_b, ALU.subtract).then_inc(tern_done, 1)
            dve.memset(zmax, -3.0e38).then_inc(zinit, 1)
            dve.memset(zmin, 3.0e38).then_inc(zinit, 1)

            def moments(b, u, src, bn_t, mv_t, bn_s, mv_s):
                for t in range(TILES):
                    last = dve.bn_stats(bn_t[:, t, :], src[:, t, :])
                last.then_inc(bn_s, 1)
                dve.wait_ge(bn_s, nth(b, u))
                hold()
                for t in range(TILES):
                    last = dve.bn_aggr(mv_t[:, t, :], bn_t[:, t, :])
                last.then_inc(mv_s, 1)
                dve.wait_ge(mv_s, nth(b, u))

            def step_a(b, u):
                if exists(b, u + 1):
                    k = (u + 1) % 2
                    dve.wait_ge(z_ready, nth(b, u + 1))
                    if exists(b, u):
                        dve.wait_ge(z_used, nth(b, u))
                    else:
                        dve.wait_ge(zinit, 2)
                    dve.tensor_tensor(zmax, zmax, z[:], ALU.max)
                    dve.tensor_tensor(zmin, zmin, z[:], ALU.min).then_inc(z_used, 1)
                    dve.tensor_copy(stat_cols(b, u + 1), stat[:, k, :]).then_inc(stat_saved, 1)
                for t in range(TILES):
                    if exists(b, u):
                        dve.wait_ge(kf_exp, nth(b, u, t + 1, 4))
                        dve.scalar_tensor_tensor(key_feat[:, t, :], pair_flat(1 + t % 2), 0.0, key_feat[:, t, :],
                                                 ALU.max, ALU.add).then_inc(kf_ready, 1)
                    if t == 0 and exists(b, u + 1):
                        dve.wait_ge(xnT_hi, nth(b, u + 1))
                        dve.tensor_tensor(xnT[1][:], pair(0), xnT[0][:].bitcast(F32), ALU.subtract).then_inc(xnT_lo, 1)
                    if t == 1 and exists(b, u + 1):
                        dve.wait_ge(kT_hi, nth(b, u + 1))
                        dve.tensor_tensor(keys[1][:, (u + 1) % 2], pair(0), keys[0][:, (u + 1) % 2].bitcast(F32),
                                          ALU.subtract).then_inc(kT_lo, 1)
                    if t == 1 and u % GPB == 0 and exists(b, u - 1):
                        dve.wait_ge(kv_mm, nth(b, u - 1, 4, 4))
                        dve.wait_ge(mask_ready, 2)
                        dve.tensor_tensor(kv_cols(b + u // GPB - 1), ps[:, 6, 0:KVW], kv_mask[:], ALU.mult).then_inc(kv_saved, 1)
                    if t == 2 and exists(b, u + 2):
                        k = u % 2
                        dve.wait_ge(x_loaded[k], dma_nth(b, u + 2))
                        moments(b, u + 2, xin[:, k], bn, mv, bn_done, mv_done)
                        if exists(b, u + 1):
                            dve.wait_ge(std_ready, nth(b, u + 1))
                        if exists(b, u):
                            dve.wait_ge(stat_saved, nth(b, u))
                            dve.wait_ge(z_ready, nth(b, u))
                        dve.tensor_scalar(stat[:, k, 8:12], mv[:, :, 0], -1.0, None, ALU.mult)
                        dve.tensor_scalar(pw[:, 0:TILES], mv[:, :, 1], EPS_LN, None, ALU.add).then_inc(ve_done, 1)
                        dve.wait_ge(ve_done, nth(b, u + 2))
                        dve.reciprocal(inv[:], pw[:, 0:TILES]).then_inc(inv_done, 1)
                        dve.wait_ge(inv_done, nth(b, u + 2))
                        dve.tensor_tensor(inv[:], inv[:], mv[:, :, 1], ALU.mult).then_inc(ratio_done, 1)
                        dve.wait_ge(ratio_done, nth(b, u + 2))
                        dve.tensor_scalar(pw[:, TILES:8], inv[:], EPS_FFN_LN, None, ALU.add).then_inc(pw_ready, 1)

            over_groups(dve, step_a)

            dve.wait_ge(z_used, GROUPS)
            zf = [zmax.rearrange("p t d -> p (t d)"), zmin.rearrange("p t d -> p (t d)")]
            for step, width in enumerate((2 * D, D)):
                for a, op in zip(zf, (ALU.max, ALU.min)):
                    last = dve.tensor_tensor(a[:, 0:width], a[:, 0:width], a[:, width:2 * width], op)
                    last.then_inc(zm_part if step == 0 else zmT_in, 1)
                dve.wait_ge(zm_part, 2)
            dve.wait_ge(zmT_mm, 1)
            dve.tensor_reduce(zext[:, 0:2], ps[:, 0, 0:256].rearrange("p (k n) -> p k n", k=2), AX_X, ALU.max)
            dve.tensor_reduce(zext[:, 2:4], ps[:, 0, 256:512].rearrange("p (k n) -> p k n", k=2), AX_X, ALU.min).then_inc(zext_done, 1)
            dve.wait_ge(zext_done, 1)
            for i in range(2):
                last = dve.tensor_tensor(zext[:, 2 * i:2 * i + 2], zext[:, 2 * i:2 * i + 2], lng_col[:], ALU.mult)
            last.then_inc(g_chain, 1)
            dve.wait_ge(g_chain, 1)
            for i in range(2):
                last = dve.tensor_tensor(zext[:, 2 * i:2 * i + 2], zext[:, 2 * i:2 * i + 2], lnb_col[:], ALU.add)
            last.then_inc(g_chain, 1)
            dve.wait_ge(g_chain, 2)
            dve.tensor_scalar(zabs, zext, -1.0, None, ALU.mult).then_inc(g_chain, 1)
            dve.wait_ge(g_chain, 3)
            dve.tensor_tensor(zabs, zabs, zext, ALU.max).then_inc(g_chain, 1)
            dve.wait_ge(g_chain, 4)
            dve.tensor_reduce(zpart, zabs, AX_X, ALU.max).then_inc(zm_done, 1)
            dve.wait_ge(zpart_mm, 1)
            dve.tensor_reduce(small[0:1, 21:22], ps[0:1, 2, 0:P], AX_X, ALU.max).then_inc(g_one, 1)
            dve.wait_ge(g_all, 1)
            dve.tensor_copy(gmax, ps[:, 4, 0:1]).then_inc(g_chain, 1)
            dve.wait_ge(g_chain, 5)
            dve.reciprocal(qscale, gmax).then_inc(g_chain, 1)
            dve.tensor_tensor(y_scale, y_scale, gmax, ALU.mult).then_inc(scales_y, 1)
            dve.wait_ge(g_chain, 6)
            dve.tensor_scalar(gz, lng_col[:], qscale, QB, ALU.mult, ALU.mult)
            dve.tensor_scalar(bz, lnb_col[:], qscale, QB, ALU.mult, ALU.mult).then_inc(scales_ready, 1)

            def step_b(b, u):
                if exists(b, u + 2):
                    k = u % 2
                    if exists(b, u):
                        dve.wait_ge(zb_ready, nth(b, u))
                    dve.tensor_copy(stat[:, k, :], stat_cols(b, u + 2)).then_inc(stat_got, 1)
                if exists(b, u):
                    dve.wait_ge(nT_hi, nth(b, u))
                    dve.tensor_tensor(tT[1][:], pair(0), tT[0][:].bitcast(F32), ALU.subtract).then_inc(nT_lo, 1)
                if exists(b, u - 1):
                    dve.wait_ge(w2_mm, nth(b, u - 1, 4, 4))
                    dve.wait_ge(res2_ready, nth(b, u - 1))
                    if exists(b, u - 2):
                        dve.wait_ge(out_ready, nth(b, u - 2))
                    dve.tensor_tensor(x2[:].rearrange("p t d -> p (t d)"), pair_flat(1), res2[:].rearrange("p t d -> p (t d)"),
                                      ALU.add).then_inc(x2_sum, 1)
                    dve.wait_ge(x2_sum, nth(b, u - 1))
                    moments(b, u - 1, x2, bn2, mv2, bn2_done, mv2_done)
                    if exists(b, u - 2):
                        dve.wait_ge(rs2_ready, nth(b, u - 2))
                    dve.tensor_scalar(ve2[:], mv2[:, :, 1], EPS_LN, None, ALU.add).then_inc(ve2_ready, 1)
                for p in range(FC // 2):
                    if exists(b, u):
                        dve.wait_ge(gelu_done, nth(b, u, p + 1, 4))
                        if exists(b, u - 1):
                            dve.wait_ge(w2_mm, nth(b, u - 1, 4, 4))
                        dve.tensor_copy(hid[0][:, 2 * p:2 * p + 2, :].rearrange("p a c -> p (a c)"), hidden[:, p % 2]).then_inc(h_hi, 1)
                    if p == 1 and exists(b, u - 1):
                        k = (u - 1) % 2
                        for t in range(TILES):
                            last = dve.scalar_tensor_tensor(x2[:, t, :], x2[:, t, :], mv2[:, t, 0:1], gamma_row[:],
                                                            ALU.subtract, ALU.mult)
                        last.then_inc(x2_scaled, 1)
                        dve.wait_ge(x2_scaled, nth(b, u - 1))
                        dve.wait_ge(rs2_ready, nth(b, u - 1))
                        dve.wait_ge(acc_ready, nth(b, u - 1))
                        for t in range(TILES):
                            last = dve.scalar_tensor_tensor(xres[:, k, t, :], x2[:, t, :], rs2[:, t:t + 1], xres[:, k, t, :],
                                                            ALU.mult, ALU.add)
                        last.then_inc(out_ready, 1)
                if exists(b, u + 1):
                    if (u + 1) % GPB == 0:
                        batch = b + (u + 1) // GPB
                        dve.wait_ge(kv_saved, B)
                        if exists(b, u):
                            dve.wait_ge(at_mm, nth(b, u, 2, 2))
                        dve.tensor_copy(kv_cur[:], kv_cols(batch)).then_inc(kv_ready, 1)
                    for p in range(HC // 2):
                        dve.wait_ge(qf_exp, nth(b, u + 1, p + 1, 4))
                        q = feat[:, 2 * p:2 * p + 2, :]
                        dve.scalar_tensor_tensor(q, pair(2 + p % 2), 0.0, q, ALU.max, ALU.add).then_inc(qf_ready, 1)
                    for a in range(2):
                        dve.wait_ge(at_mm, nth(b, u + 1, a + 1, 2))
                        if exists(b, u):
                            dve.wait_ge(aT_mm, nth(b, u))
                            dve.wait_ge(zs_lo, nth(b, u))
                        sums = ps[:, 4 + 2 * a:6 + 2 * a, 0:KVW].rearrange("p t (h e) -> p t h e", e=VW)
                        r = rden[:, 2 * a:2 * a + 2, :]
                        dve.tensor_scalar(r, sums[:, :, :, HD], EPS_ATTN * KV_SCALE, None, ALU.add).then_inc(den_done, 1)
                        dve.wait_ge(den_done, nth(b, u + 1, a + 1, 2))
                        dve.reciprocal(r, r).then_inc(rden_done, 1)
                        dve.wait_ge(rden_done, nth(b, u + 1, a + 1, 2))
                        dve.tensor_tensor(attn[:, 2 * a:2 * a + 2, :].rearrange("p t (h e) -> p t h e", e=HD),
                                          sums[:, :, :, 0:HD], r.unsqueeze(3).broadcast_to([P, 2, H, HD]),
                                          ALU.mult).then_inc(at_ready, 1)
                if exists(b, u):
                    k = u % 2
                    dve.wait_ge(y_mm, nth(b, u))
                    dve.wait_ge(xb_ready, nth(b, u))
                    dve.scalar_tensor_tensor(xres[:, k].rearrange("p t d -> p (t d)"), pair_flat(0), y_scale,
                                             xres[:, k].rearrange("p t d -> p (t d)"), ALU.mult, ALU.add).then_inc(acc_ready, 1)
                if exists(b, u + 1):
                    dve.wait_ge(aT_hi, nth(b, u + 1))
                    dve.tensor_tensor(tT[1][:], pair(2), tT[0][:].bitcast(F32), ALU.subtract).then_inc(aT_lo, 1)
                    dve.wait_ge(zq_affine, nth(b, u + 1))
                    dve.tensor_scalar(zq, zq, CLIP, -CLIP, ALU.min, ALU.max).then_inc(zq_clipped, 1)
                    dve.wait_ge(wo_mm, nth(b, u + 1))
                    dve.wait_ge(res1_ready, nth(b, u + 1))
                    if exists(b, u):
                        dve.wait_ge(nT_mm, nth(b, u))
                        dve.wait_ge(res2_ready, nth(b, u))
                    dve.tensor_tensor(n1[:].rearrange("p t d -> p (t d)"), pair_flat(3), res1[:].rearrange("p t d -> p (t d)"),
                                      ALU.add).then_inc(x1_sum, 1)
                    dve.wait_ge(x1_sum, nth(b, u + 1))
                    moments(b, u + 1, n1, bn1, mv1, bn1_done, mv1_done)
                    if exists(b, u):
                        dve.wait_ge(rs1_ready, nth(b, u))
                    dve.tensor_scalar(ve1[:], mv1[:, :, 1], EPS_LN, None, ALU.add).then_inc(ve1_ready, 1)
                if exists(b, u + 2):
                    dve.wait_ge(xT_hi, nth(b, u + 2))
                    dve.tensor_tensor(xnT[1][:], pair(2), xnT[0][:].bitcast(F32), ALU.subtract).then_inc(xT_lo, 1)
                if exists(b, u + 1):
                    dve.wait_ge(rs1_ready, nth(b, u + 1))
                    for t in range(TILES):
                        last = dve.tensor_scalar(n1[:, t, :], n1[:, t, :], mv1[:, t, 0:1], rs1[:, t:t + 1], ALU.subtract, ALU.mult)
                    last.then_inc(n1_ready, 1)
                if exists(b, u + 2):
                    dve.wait_ge(qT_hi, nth(b, u + 2))
                    dve.tensor_tensor(qT[1][:], pair(3), qT[0][:].bitcast(F32), ALU.subtract).then_inc(qT_lo, 1)

            over_groups(dve, step_b)

        @block.tensor
        def _(pe):
            pe.wait_ge(consts_set, 4)
            done = 0
            for n, s in enumerate(WEIGHT_SLOTS):
                if n == 0:
                    pe.wait_ge(ld_qkv, 32)
                if n == 2:
                    pe.wait_ge(ld_w1, 16)
                if n == 4:
                    pe.wait_ge(ld_w2, 16)
                    pe.wait_ge(wT_lo, 2)
                for col, src in weight_blocks(n):
                    last = pe.transpose(pair_flat(s)[:, col:col + P], src, ident[:])
                last.then_inc(wT_mm, 1)
            pe.wait_ge(w1_plain, 2)
            pe.wait_ge(ld_cols, 16 * 5)
            for c in range(FC):
                for d in range(KD):
                    last = pe.matmul(ps[:, 4, c:c + 1], w1T[:, d, c * P:(c + 1) * P], beta_col[:, d:d + 1],
                                     start=(c == 0 and d == 0), stop=(c == FC - 1 and d == KD - 1), skip_group_check=True)
            last.then_inc(b1_mm, 1)
            pe.wait_ge(w_abs, 1)
            pe.matmul(ps[:, 5, 0:1], ones[:], colsum, start=True, stop=True).then_inc(w_sum, 1)
            pe.wait_ge(wT_lo, 5)
            pe.wait_ge(proj_lo, 1)
            pe.wait_ge(b1_done, 1)
            pe.wait_ge(tern_done, 1)

            def transposes(dst, src):
                for c in range(KD):
                    for t in range(TILES):
                        last = pe.transpose(dst[:, c, tile_cols(t)], src[:, t, tile_cols(c)], ident[:])
                return last

            def step_a(b, u):
                for t in range(TILES):
                    if exists(b, u):
                        s = 1 + t % 2
                        if t == 0:
                            pe.wait_ge(kT_lo, nth(b, u))
                        if t >= 2:
                            pe.wait_ge(kf_ready, nth(b, u, t - 1, 4))
                        elif exists(b, u - 1):
                            pe.wait_ge(kf_ready, nth(b, u - 1, t + 3, 4))
                        for hg in range(KD):
                            last = three_passes(pe, ps[:, 2 * s + hg, :],
                                                lambda c: tuple(part[:, u % 2, c, tile_cols(t)] for part in keys),
                                                columns(projs, slice(None)), [hg])
                        last.then_inc(kf_mm, 1)
                    if exists(b, u + 1):
                        if t == 0:
                            pe.wait_ge(xn_ready, nth(b, u + 1))
                            if exists(b, u):
                                pe.wait_ge(v_ready, nth(b, u))
                            transposes(pair(0), xin[:, (u + 1) % 2]).then_inc(xnT_mm, 1)
                        if t == 1:
                            pe.wait_ge(xnT_lo, nth(b, u + 1))
                            for m in range(KD):
                                last = three_passes(pe, ps[:, m, :], columns(wk, tile_cols(m)), columns(xnT, slice(None)), range(KD))
                            last.then_inc(kT_mm, 1)
                        if t == 2:
                            pe.wait_ge(kT_lo, nth(b, u + 1))
                            for i in range(TILES):
                                last = three_passes(pe, pair_flat(0)[:, i * D:(i + 1) * D], columns(xnT, tile_cols(i)),
                                                    columns(wv, slice(None)), range(KD))
                            last.then_inc(v_mm, 1)
                    w, i = (u - 1, t + 2) if t < 2 else (u, t - 2)
                    if exists(b, w):
                        pe.wait_ge(kf_ready, nth(b, w, i + 1, 4))
                        if i == 0:
                            pe.wait_ge(v_ready, nth(b, w))
                            if w % GPB == 0 and exists(b, w - 1):
                                pe.wait_ge(kv_saved, b + w // GPB)
                        for c in range(HC):
                            first = w % GPB == 0 and i == 0 and c == 0
                            end = w % GPB == GPB - 1 and i == TILES - 1 and c == HC - 1
                            last = pe.matmul(ps[:, 6, c * CW:(c + 1) * CW], key_feat[:, i, c * P:(c + 1) * P],
                                             vals[:, w % 2, i, c * CW:(c + 1) * CW], start=first, stop=end, skip_group_check=True)
                        last.then_inc(kv_mm, 1)

            over_groups(pe, step_a)

            pe.wait_ge(zmT_in, 2)
            pe.wait_ge(v_ready, GROUPS)
            for n, a in enumerate((zmax, zmin)):
                for c in range(KD):
                    col = (n * KD + c) * P
                    last = pe.transpose(ps[:, 0, col:col + P], a.rearrange("p t d -> p (t d)")[:, c * P:(c + 1) * P], ident[:])
            last.then_inc(zmT_mm, 1)
            pe.wait_ge(zm_done, 1)
            pe.transpose(ps[0:1, 2, 0:P], zpart, ident[:]).then_inc(zpart_mm, 1)
            pe.wait_ge(g_one, 1)
            pe.matmul(ps[:, 4, 0:1], ones[0:1, :], small[0:1, 21:22], start=True, stop=True).then_inc(g_all, 1)
            pe.wait_ge(scales_ready, 1)
            pe.wait_ge(kv_saved, B)

            def step_b(b, u):
                def query_features(p):
                    if p == 0:
                        pe.wait_ge(qT_lo, nth(b, u + 1))
                    else:
                        if p >= 2:
                            pe.wait_ge(qf_ready, nth(b, u + 1, p - 1, 4))
                    for a in range(2):
                        c = 2 * p + a
                        last = three_passes(pe, ps[:, 4 + 2 * (p % 2) + a, :],
                                            lambda k: tuple(part[:, k, tile_cols(c % 4)] for part in projs),
                                            columns(qT, slice(None)), [c // 4])
                    last.then_inc(qf_mm, 1)

                def out_tile(t):
                    if t == 0:
                        pe.wait_ge(h_lo, nth(b, u, 4, 4))
                        pe.wait_ge(gelu_done, nth(b, u, 3, 4))
                    three_passes(pe, pair_flat(1)[:, t * D:(t + 1) * D], columns(hid, tile_cols(t)),
                                 columns(w2s, slice(None)), range(FC)).then_inc(w2_mm, 1)

                if exists(b, u):
                    pe.wait_ge(n1_ready, nth(b, u))
                    pe.wait_ge(zq_affine, nth(b, u))
                    transposes(pair(0), n1).then_inc(nT_mm, 1)
                    for p in range(FC // 2):
                        if p == 0:
                            pe.wait_ge(nT_lo, nth(b, u))
                            if exists(b, u - 1):
                                pe.wait_ge(x2_sum, nth(b, u - 1))
                        if p >= 2:
                            pe.wait_ge(gelu_done, nth(b, u, p - 1, 4))
                        for a in range(2):
                            c = 2 * p + a
                            last = three_passes(pe, ps[:, 2 * ((p + 1) % 2) + a, :], columns(w1s, tile_cols(c)),
                                                columns(tT, slice(None)), range(KD))
                        last.then_inc(w1_mm, 1)
                for p in range(HC // 2):
                    if exists(b, u + 1):
                        query_features(p)
                    if exists(b, u) and p in (0, 1, 3):
                        out_tile((0, 1, None, 2)[p])
                if exists(b, u + 1):
                    for t in range(TILES):
                        if t == 0:
                            pe.wait_ge(qf_ready, nth(b, u + 1, 4, 4))
                            pe.wait_ge(kv_ready, b + (u + 1) // GPB + 1)
                        for c in range(HC):
                            last = pe.matmul(ps[:, 4 + t, c * CW:(c + 1) * CW], feat[:, c, tile_cols(t)],
                                             kv_cur[:, c * CW:(c + 1) * CW], start=(c == 0), stop=(c == HC - 1), skip_group_check=True)
                        if t % 2:
                            last.then_inc(at_mm, 1)
                if exists(b, u):
                    pe.wait_ge(zs_lo, nth(b, u))
                    pe.wait_ge(gelu_done, nth(b, u, 4, 4))
                    for t in range(TILES):
                        steps = [(c, part) for c in range(KD) for part in zs]
                        for n, (c, part) in enumerate(steps):
                            last = pe.matmul(pair_flat(0)[:, t * D:(t + 1) * D], part[:, c, tile_cols(t)], ternary[:, c, :],
                                             start=(n == 0), stop=(n == len(steps) - 1))
                    last.then_inc(y_mm, 1)
                if exists(b, u + 1):
                    pe.wait_ge(at_ready, nth(b, u + 1, 2, 2))
                    transposes(pair(2), attn).then_inc(aT_mm, 1)
                    pe.wait_ge(zb_ready, nth(b, u + 1))
                    if exists(b, u):
                        pe.wait_ge(acc_ready, nth(b, u))
                    transposes(pair(0), z).then_inc(zT_mm, 1)
                    pe.wait_ge(aT_lo, nth(b, u + 1))
                    for t in range(TILES):
                        last = three_passes(pe, pair_flat(3)[:, t * D:(t + 1) * D], columns(tT, tile_cols(t)),
                                            columns(wo, slice(None)), range(KD))
                    last.then_inc(wo_mm, 1)
                if exists(b, u + 2):
                    pe.wait_ge(xnb_ready, nth(b, u + 2))
                    transposes(pair(2), xin[:, u % 2]).then_inc(xT_mm, 1)
                    pe.wait_ge(xT_lo, nth(b, u + 2))
                    if exists(b, u + 1):
                        pe.wait_ge(x1_sum, nth(b, u + 1))
                    for m in range(KD):
                        last = three_passes(pe, ps[:, 6 + m, :], columns(wq, tile_cols(m)), columns(xnT, slice(None)), range(KD))
                    last.then_inc(qT_mm, 1)
                if exists(b, u):
                    out_tile(3)

            over_groups(pe, step_b)


_INS = ['L0_attn_x', 'L0_attn_proj', 'L0_attn_w_qkv', 'L0_attn_w_out', 'L0_attn_b_out', 'L0_attn_gamma', 'L0_attn_beta',
        'L0_attn_w1', 'L0_attn_b1', 'L0_attn_w2', 'L0_attn_b2', 'L0_ffn_weight', 'L0_ffn_ln_gamma', 'L0_ffn_ln_beta']
_OUTS = [((B, N, D), 'float32')]


def kernel(**inputs):
    import numpy as _np
    import concourse.bacc as _bacc
    from concourse import mybir as _mybir
    from concourse.bass_utils import run_bass_kernel_spmd as _run

    nc = _bacc.Bacc("TRN2", target_bir_lowering=False, num_devices=1)
    arrays, args = {}, []
    for name in _INS:
        a = _np.ascontiguousarray(inputs[name])
        arrays[f"in_{name}_dram"] = a
        args.append(nc.dram_tensor(f"in_{name}_dram", a.shape, _mybir.dt.from_np(a.dtype), kind="ExternalInput").ap())
    for i, (shape, dtype) in enumerate(_OUTS):
        dt = _mybir.dt.from_np(_np.dtype(dtype))
        args.append(nc.dram_tensor(f"out_{i}_dram", shape, dt, kind="ExternalOutput").ap())
    linear_attention_block(nc, *args)
    r = _run(nc, [arrays], core_ids=[0])
    got = tuple(r.results[0][f"out_{i}_dram"] for i in range(len(_OUTS)))
    return got[0]
```

```python
from contextlib import ExitStack

import concourse.bass as bass
from concourse import mybir

F32 = mybir.dt.float32
F32R = mybir.dt.float32r
F16 = mybir.dt.float16
ALU = mybir.AluOpType
ACT = mybir.ActivationFunctionType
AX_X = mybir.AxisListType.X

P = 128
B, N, D = 8, 2048, 256
H, HD, F = 16, 16, 64
FF = 4 * D
TILES = 4
GT = TILES * P
GPB = N // GT
GROUPS = B * GPB
KD = D // P
HC = H * F // P
FC = FF // P
VW = HD + 1
CW = 2 * VW
KVW = HC * CW
PAIR = 2 * 512

EPS_LN = 1e-5
EPS_ATTN = 1e-8
EPS_FFN_LN = 1e-3
EPS_FFN = 1e-5
QB = 128.0
CLIP = QB - EPS_FFN
PASSES = (0, 0), (0, 1), (1, 0)
PAIR_D = 2 * HD
STACK = len(PASSES) * PAIR_D
KV_SCALE = 1.0 / N


def nth(b, u, j=1, per=1):
    return b * (GPB * per) + (per * u + j)


def exists(b, u):
    return not isinstance(b, int) or 0 <= GPB * b + u < GROUPS


def dma_nth(b, u):
    return b * (16 * GPB // 2) + 16 * ((u - u % 2) // 2 + 1)


def over_groups(eng, step):
    for u in range(-3, GPB):
        step(0, u)
    with eng.Fori(1, B - 1) as b:
        for u in range(GPB):
            step(b, u)
    for u in range(GPB + 1):
        step(B - 1, u)


def linear_attention_block(nc, x, proj, w_qkv, w_out, b_out, gamma, beta, w1, b1, w2, b2,
                           ffn_weight, ln_gamma, ln_beta, out):
    x_rows = x.rearrange("b n d -> (b n) d").rearrange("(g p t) d -> g p t d", p=P, t=TILES)
    out_rows = out.rearrange("b n d -> (b n) d").rearrange("(g p t) d -> g p t d", p=P, t=TILES)

    with ExitStack() as ctx:
        def sb(name, shape, dt=F32):
            return ctx.enter_context(nc.sbuf_tensor(name, shape, dt))

        def sem(name):
            return ctx.enter_context(nc.semaphore(name))

        ps = ctx.enter_context(nc.psum_tensor("ps", [P, 8, 512], F32))

        def pair(s):
            return ps[:, 2 * s:2 * s + 2, :]

        def pair_flat(s):
            return pair(s).rearrange("p a b -> p (a b)")

        ident = sb("ident", [P, P])
        ones = sb("ones", [P, P])
        minus_half = sb("minus_half", [P, 8])

        def split(name, shape):
            return sb(name + "_hi", shape, F32R), sb(name + "_lo", shape, F32R)

        wq = split("wq", [P, KD, D])
        wkv = split("wkv", [P, KD, 2 * D])
        wk, wv = (tuple(w[:, :, i * D:(i + 1) * D] for w in wkv) for i in range(2))
        wo = split("wo", [P, KD, D])
        w1s = split("w1s", [P, KD, FF])
        w2s = split("w2s", [P, FC, D])
        proj_room = sb("proj_room", [P, 2, KD, 8 * F], F32R)
        projs = proj_room[:, 0], proj_room[:, 1]
        proj_stack = sb("proj_stack", [P, HC, P], F16)
        ternary = sb("ternary", [P, KD, D], F32R)
        gamma_row, beta_row, bout_row, b2_row = (sb(n, [P, D]) for n in ("gamma_row", "beta_row", "bout_row", "b2_row"))
        gamma_col, beta_col, lng_col, lnb_col = (sb(n, [P, KD]) for n in ("gamma_col", "beta_col", "lng_col", "lnb_col"))
        b1_col = sb("b1_col", [P, FC])
        small = sb("small", [P, 32])
        w_mean, w_half, w_minus_half, gmax, qscale, y_scale, colsum = (small[:, i:i + 1] for i in range(7))
        gz, bz = small[:, 8:10], small[:, 10:12]
        zext, zabs, zpart = small[:, 12:16], small[:, 16:20], small[:, 20:21]

        xin = sb("xin", [P, 2, TILES, D])
        z = sb("z", [P, TILES, D])
        xnT = split("xnT", [P, KD, GT])
        feat = sb("feat", [P, 2, PAIR])
        fs = sb("fs_hi", [P, HC * 512], F16), sb("fs_lo", [P, HC * 512], F16)
        hf = sb("hf", [P, 2 * TILES * KVW])
        hid = split("hid", [P, FC, GT])
        xres = sb("xres", [P, 2, TILES, D])
        stats = sb("stats", [P, GROUPS * 12])
        stat = sb("stat", [P, 2, 12])
        kv_all = sb("kv_all", [P, B * 2 * KVW], F16)
        kv_buf = sb("kv_buf", [P, KVW])
        kv_mask, kv_cur = kv_buf, kv_buf[:].bitcast(F16)
        qT = sb("qT_hi", [P, KD, GT], F16), sb("qT_lo", [P, KD, GT], F16)
        attn = sb("attn", [P, TILES, D])
        tT = split("tT", [P, KD, GT])
        n1 = sb("n1", [P, TILES, D])
        res1 = sb("res1", [P, TILES, D])
        res2 = sb("res2", [P, TILES, D])
        x2 = sb("x2", [P, TILES, D])
        zq = attn.rearrange("p t d -> p (t d)").rearrange("p (k t) -> p k t", k=KD)
        zs = wkv
        bn = sb("bn", [P, TILES, 6])
        mv = sb("mv", [P, TILES, 2])
        pw = sb("pw", [P, 8])
        inv = sb("inv", [P, TILES])
        mv1, mv2 = sb("mv1", [P, TILES, 2]), sb("mv2", [P, TILES, 2])
        bn1, bn2 = sb("bn1", [P, TILES, 6]), sb("bn2", [P, TILES, 6])
        ve1, ve2 = sb("ve1", [P, TILES]), sb("ve2", [P, TILES])
        rs1, rs2 = sb("rs1", [P, TILES]), sb("rs2", [P, TILES])
        rden = sb("rden", [P, TILES, H])

        keys = tuple(part[:, 0:2 * KD, :].rearrange("p (k c) t -> p k c t", k=2) for part in hid)
        key_feat = [feat[:, 0, :], feat[:, 1, :], n1.rearrange("p t d -> p (t d)"), res1.rearrange("p t d -> p (t d)")]
        key_fs = [f.rearrange("p (t c) -> p t c", t=TILES) for f in fs]
        query_fs = [f.rearrange("p (c t) -> p c t", c=HC) for f in fs]
        vals = hf[:].bitcast(F16).rearrange("p (i k t c) -> p i k t c", i=2, k=2, t=TILES)
        q_stack = proj_room.rearrange("p i k c -> p (i k c)").bitcast(F16).rearrange("p (c t) -> p c t", c=HC)
        raw_stack = z.rearrange("p t d -> p (t d)").rearrange("p (c f) -> p c f", c=HC)
        kv_new = x2.rearrange("p t d -> p (t d)")[:, 0:KVW]
        hidden = hf[:, 0:2 * PAIR].rearrange("p (k c) -> p k c", k=2)
        zmax, zmin = xres[:, 0], xres[:, 1]
        raw_w1 = feat.rearrange("p a c -> p (a c)").rearrange("p (r d) -> p r d", d=D)
        raw_w2 = fs[0][:].bitcast(F32).rearrange("p (r f) -> p r f", f=FF)
        raw_qkv = xin.rearrange("p k t d -> p (k t) d")[:, 0:6, :]
        raw_out = xin.rearrange("p k t d -> p (k t) d")[:, 6:8, :]
        raw_proj = attn.rearrange("p t d -> p (t d)").rearrange("p (k c) -> p k c", k=KD)
        raw_ffn = n1[:, 0:2, :]
        w1T = xres.rearrange("p k t d -> p k (t d)")
        tern_a, tern_b = res1.rearrange("p t d -> p (t d)")[:, 0:KD * D], res2.rearrange("p t d -> p (t d)")[:, 0:KD * D]

        consts_set, proj_zero, mask_zero, mask_ready = sem("consts_set"), sem("proj_zero"), sem("mask_zero"), sem("mask_ready")
        ld_qkv, ld_w1, ld_w2, ld_ffn, ld_proj, ld_cols, ld_rows = (
            sem(n) for n in ("ld_qkv", "ld_w1", "ld_w2", "ld_ffn", "ld_proj", "ld_cols", "ld_rows"))
        wT_mm, wT_hi, wT_lo = sem("wT_mm"), sem("wT_hi"), sem("wT_lo")
        w1_plain, w1_scaled, b1_mm, b1_done = sem("w1_plain"), sem("w1_scaled"), sem("b1_mm"), sem("b1_done")
        w_abs, w_sum, w_chain, tern_done = sem("w_abs"), sem("w_sum"), sem("w_chain"), sem("tern_done")
        proj_hi, proj_lo = sem("proj_hi"), sem("proj_lo")
        ld_stack, stack_hi, stack_lo, q_stacked = sem("ld_stack"), sem("stack_hi"), sem("stack_lo"), sem("q_stacked")
        vals_ones, zinit = sem("vals_ones"), sem("zinit")

        x_loaded = [sem("x_loaded0"), sem("x_loaded1")]
        bn_done, mv_done, ve_done, inv_done, ratio_done, pw_ready = (
            sem(n) for n in ("bn_done", "mv_done", "ve_done", "inv_done", "ratio_done", "pw_ready"))
        std_ready, xn_ready, z_used, stat_saved = (
            sem(n) for n in ("std_ready", "xn_ready", "z_used", "stat_saved"))
        xnT_mm, xnT_hi, xnT_lo = sem("xnT_mm"), sem("xnT_hi"), sem("xnT_lo")
        kT_mm, kT_hi, kT_lo = sem("kT_mm"), sem("kT_hi"), sem("kT_lo")
        v_mm, v_ready = sem("v_mm"), sem("v_ready")
        kf_mm, kf_neg, kf_exp, kf_ready = sem("kf_mm"), sem("kf_neg"), sem("kf_exp"), sem("kf_ready")
        kf_hi, kf_lo, v_hi = sem("kf_hi"), sem("kf_lo"), sem("v_hi")
        kv_mm, kv_new_done, kv_hi, kv_saved = sem("kv_mm"), sem("kv_new_done"), sem("kv_hi"), sem("kv_saved")

        pool_held, dve_held = sem("pool_held"), sem("dve_held")
        zmT_in, scales_y = sem("zmT_in"), sem("scales_y")
        zm_part, zm_done, zmT_mm, zext_done, g_chain, zpart_mm, g_one, g_all, scales_ready = (
            sem(n) for n in ("zm_part", "zm_done", "zmT_mm", "zext_done", "g_chain", "zpart_mm", "g_one", "g_all", "scales_ready"))

        x2_loaded = [sem("x2_loaded0"), sem("x2_loaded1")]
        r_loaded = [sem("r_loaded0"), sem("r_loaded1")]
        stored = [sem("stored0"), sem("stored1")]
        stat_got, xnb_ready, zb_ready, res1_ready = (sem(n) for n in ("stat_got", "xnb_ready", "zb_ready", "res1_ready"))
        kv_ready = sem("kv_ready")
        xT_mm, xT_hi, xT_lo = sem("xT_mm"), sem("xT_hi"), sem("xT_lo")
        qT_mm, qT_hi, qT_lo = sem("qT_mm"), sem("qT_hi"), sem("qT_lo")
        qf_mm, qf_neg, qf_exp, qf_ready = sem("qf_mm"), sem("qf_neg"), sem("qf_exp"), sem("qf_ready")
        qf_hi, qf_lo_dve, qf_lo_pool = sem("qf_hi"), sem("qf_lo_dve"), sem("qf_lo_pool")
        h_lo_dve = sem("h_lo_dve")
        at_mm, den_done, rden_done, at_ready = sem("at_mm"), sem("den_done"), sem("rden_done"), sem("at_ready")
        aT_mm, aT_hi, aT_lo = sem("aT_mm"), sem("aT_hi"), sem("aT_lo")
        wo_mm, x1_sum, bn1_done, mv1_done, ve1_ready, rs1_ready, n1_ready = (
            sem(n) for n in ("wo_mm", "x1_sum", "bn1_done", "mv1_done", "ve1_ready", "rs1_ready", "n1_ready"))
        res2_part, res2_ready = sem("res2_part"), sem("res2_ready")
        nT_mm, nT_hi, nT_lo = sem("nT_mm"), sem("nT_hi"), sem("nT_lo")
        w1_mm, gelu_done, h_hi, h_lo, w2_mm = (sem(n) for n in ("w1_mm", "gelu_done", "h_hi", "h_lo", "w2_mm"))
        x2_sum, bn2_done, mv2_done, ve2_ready, rs2_ready, x2_scaled, out_ready = (
            sem(n) for n in ("x2_sum", "bn2_done", "mv2_done", "ve2_ready", "rs2_ready", "x2_scaled", "out_ready"))
        zT_mm, zq_affine, zq_clipped, zs_hi, zs_lo, y_mm, xb_ready, acc_ready = (
            sem(n) for n in ("zT_mm", "zq_affine", "zq_clipped", "zs_hi", "zs_lo", "y_mm", "xb_ready", "acc_ready"))

        def three_passes(pe, dst, weights, moving, chunks, first=True, last=True):
            steps = [(c, i, j) for c in chunks for i, j in PASSES]
            for n, (c, i, j) in enumerate(steps):
                mm = pe.matmul(dst, weights(c)[i], moving(c)[j], start=first and n == 0,
                               stop=last and n == len(steps) - 1)
            return mm

        def columns(parts, cols):
            return lambda c: tuple(p[:, c, cols] for p in parts)

        def tile_cols(t):
            return slice(t * P, (t + 1) * P)

        def group(b, u):
            return b * GPB + u

        def stat_cols(b, u):
            return stats[:, bass.ds(group(b, u) * 12, 12)]

        def kv_cols(b):
            return kv_all[:, bass.ds(b * (2 * KVW), 2 * KVW)]

        WEIGHT_SLOTS = (0, 1, 2, 3, 0, 1)

        def weight_blocks(n):
            if n < 2:
                raws = ((raw_qkv, 0), (raw_qkv, 2)) if n == 0 else ((raw_qkv, 4), (raw_out, 0))
                return [((2 * i + c) * D + r * P, raw[:, base + r, tile_cols(c)])
                        for i, (raw, base) in enumerate(raws) for c in range(KD) for r in range(2)]
            if n < 4:
                return [(r * P, raw_w1[:, r, tile_cols(n - 2)]) for r in range(FC)]
            return [(j * D + r * P, raw_w2[:, r, tile_cols(4 * (n - 4) + j)]) for j in range(4) for r in range(2)]

        def weight_parts(n, part):
            if n < 2:
                return [(w[part][:, :, :], ps[:, 2 * n + i, :].rearrange("p (k d) -> p k d", k=KD))
                        for i, w in enumerate(((wq, wk), (wv, wo))[n])]
            return [(w2s[part][:, 4 * (n - 4):4 * (n - 3), :].rearrange("p k d -> p (k d)"), pair_flat(WEIGHT_SLOTS[n]))]

        def head_values(part, k, i):
            return vals[:, part, k, 2 * i:2 * i + 2].rearrange("p t (h e) -> p (t h) e", e=VW)[:, :, 0:HD]

        def stack_rows(eng, stack, rows, j, done):
            for r in range(P // PAIR_D):
                eng.dma_start(stack[j * PAIR_D:(j + 1) * PAIR_D, r::P // PAIR_D, :], rows(r)).then_inc(done, 16)

        def raw_proj_blocks(r):
            return raw_proj[r * PAIR_D:(r + 1) * PAIR_D, :, r * P:(r + 1) * P]

        block = ctx.enter_context(nc.Block())

        @block.sync
        def _(sp):
            sp.dma_start(raw_qkv, w_qkv.rearrange("(r p) d -> p r d", p=P)).then_inc(ld_qkv, 16)
            sp.dma_start(raw_out, w_out.rearrange("(r p) d -> p r d", p=P)).then_inc(ld_qkv, 16)
            sp.dma_start(raw_w1, w1.rearrange("(r p) d -> p r d", p=P)).then_inc(ld_w1, 16)
            sp.dma_start(raw_w2, w2.rearrange("(r p) f -> p r f", p=P)).then_inc(ld_w2, 16)
            sp.dma_start(raw_ffn, ffn_weight.rearrange("(k p) u -> p k u", p=P)).then_inc(ld_ffn, 16)
            for dst, src in ((gamma_col, gamma), (beta_col, beta), (lng_col, ln_gamma), (lnb_col, ln_beta), (b1_col, b1)):
                sp.dma_start(dst[:], src.rearrange("(k p) -> p k", p=P), allow_slow_non_contiguous=True).then_inc(ld_cols, 16)
            for dst, src in ((gamma_row, gamma), (beta_row, beta), (bout_row, b_out), (b2_row, b2)):
                sp.dma_start(dst[:], src.partition_broadcast(P)).then_inc(ld_rows, 16)
            sp.wait_ge(proj_zero, 1)
            for h in range(H):
                r = h % 8
                sp.dma_start(raw_proj[r * HD:(r + 1) * HD, h // 8, r * F:(r + 1) * F], proj[h]).then_inc(ld_proj, 16)
            sp.wait_ge(ld_proj, 16 * H)
            for j in range(3):
                stack_rows(sp, raw_stack, raw_proj_blocks, j, ld_stack)
            sp.wait_ge(wT_mm, 2)

            def load_a(b, u):
                if not exists(b, u + 3):
                    return
                if exists(b, u + 1):
                    sp.wait_ge(xnT_mm, nth(b, u + 1))
                    sp.wait_ge(z_used, nth(b, u + 1))
                k = (u + 1) % 2
                sp.dma_start(xin[:, k], x_rows[group(b, u + 3)]).then_inc(x_loaded[k], 16)

            over_groups(sp, load_a)
            sp.wait_ge(xnT_mm, GROUPS)
            sp.wait_ge(z_used, GROUPS)
            sp.wait_ge(kf_mm, TILES * GROUPS)

            def move_b(b, u):
                k = u % 2
                if exists(b, u + 2):
                    for part, places in ((0, (0, 2)), (1, (1,))):
                        sp.wait_ge((qT_hi, qT_lo)[part], nth(b, u + 2))
                        for j in places:
                            stack_rows(sp, q_stack, lambda r: qT[part][r * PAIR_D:(r + 1) * PAIR_D, :, :], j, q_stacked)
                if exists(b, u + 3):
                    if exists(b, u + 1):
                        sp.wait_ge(xT_mm, nth(b, u + 1))
                        sp.wait_ge(res1_ready, nth(b, u + 1))
                        sp.wait_ge(zb_ready, nth(b, u + 1))
                    sp.dma_start(xin[:, 1 - k], x_rows[group(b, u + 3)]).then_inc(x2_loaded[1 - k], 16)
                if exists(b, u - 1):
                    sp.wait_ge(out_ready, nth(b, u - 1))
                    sp.dma_start(out_rows[group(b, u - 1)], xres[:, 1 - k]).then_inc(stored[1 - k], 16)
                if exists(b, u + 1):
                    if exists(b, u - 1):
                        sp.wait_ge(stored[1 - k], dma_nth(b, u - 1))
                    else:
                        sp.wait_ge(zm_done, 1)
                    sp.dma_start(xres[:, 1 - k], x_rows[group(b, u + 1)]).then_inc(r_loaded[1 - k], 16)

            over_groups(sp, move_b)
            for s in stored:
                sp.wait_ge(s, 16 * GROUPS // 2)

        @block.gpsimd
        def _(pool):
            def hold():
                pool.sem_inc(pool_held, 1)

            def flat(a):
                return a.rearrange("p t d -> p (t d)")

            def rows4(row):
                return row[:].unsqueeze(1).broadcast_to([P, TILES, D])

            pool.memset(ones[:], 1.0).then_inc(consts_set, 1)
            pool.memset(minus_half[:], -0.5).then_inc(consts_set, 1)
            pool.memset(ident[:], 0.0).then_inc(consts_set, 1)
            pool.wait_ge(consts_set, 3)
            pool.affine_select(out=ident[:], in_=ident[:], compare_op=ALU.not_equal, fill=1.0, base=0,
                               pattern=[[-1, P]], channel_multiplier=1).then_inc(consts_set, 1)

            def norm_a(b, u):
                k = u % 2

                def low(w, t):
                    if exists(b, w):
                        pool.wait_ge(kf_hi, nth(b, w, t + 1, 4))
                        if exists(b, w - 1):
                            pool.wait_ge(kv_mm, nth(b, w - 1, t + 1, 4))
                        pool.tensor_tensor(key_fs[1][:, t, :], key_feat[t], key_fs[0][:, t, :], ALU.subtract).then_inc(kf_lo, 1)

                if exists(b, u + 2):
                    pool.wait_ge(pw_ready, nth(b, u + 2))
                    pool.tensor_tensor(stat[:, k, 0:8], pw[:], minus_half[:], ALU.pow).then_inc(std_ready, 1)
                low(u - 1, 3)
                if exists(b, u + 2):
                    pool.wait_ge(std_ready, nth(b, u + 2))
                    hold()
                    for t in range(TILES):
                        last = pool.tensor_scalar(xin[:, k, t, :], xin[:, k, t, :], stat[:, k, 8 + t:9 + t],
                                                  stat[:, k, t:t + 1], ALU.add, ALU.mult)
                    last.then_inc(xn_ready, 1)
                for t in range(3):
                    low(u, t)

            over_groups(pool, norm_a)
            pool.wait_ge(z_used, GROUPS)
            pool.wait_ge(xnT_mm, GROUPS)
            pool.wait_ge(stack_lo, 1)

            def step_b(b, u):
                if exists(b, u - 1):
                    pool.wait_ge(ve2_ready, nth(b, u - 1))
                    pool.tensor_tensor(rs2[:], ve2[:], minus_half[:, 0:TILES], ALU.pow).then_inc(rs2_ready, 1)
                if exists(b, u):
                    pool.wait_ge(n1_ready, nth(b, u))
                    if exists(b, u - 1):
                        pool.wait_ge(x2_sum, nth(b, u - 1))
                    pool.tensor_tensor(res2[:], n1[:], rows4(gamma_row), ALU.mult).then_inc(res2_part, 1)
                    pool.wait_ge(res2_part, nth(b, u))
                    pool.tensor_tensor(res2[:], res2[:], rows4(b2_row), ALU.add).then_inc(res2_ready, 1)
                    for p in range(3):
                        pool.wait_ge(h_hi, nth(b, u, p + 1, 4))
                        if exists(b, u - 1):
                            pool.wait_ge(w2_mm, nth(b, u - 1, 4, 4))
                        pool.tensor_tensor(flat(hid[1][:, 2 * p:2 * p + 2, :]), hidden[:, p % 2],
                                           flat(hid[0][:, 2 * p:2 * p + 2, :]).bitcast(F32), ALU.subtract).then_inc(h_lo, 1)
                if exists(b, u + 3):
                    k = (u + 3) % 2
                    pool.wait_ge(x2_loaded[k], dma_nth(b, u + 3))
                    pool.wait_ge(stat_got, nth(b, u + 3))
                    hold()
                    for t in range(TILES):
                        last = pool.tensor_scalar(xin[:, k, t, :], xin[:, k, t, :], stat[:, k, 8 + t:9 + t],
                                                  stat[:, k, t:t + 1], ALU.add, ALU.mult)
                    last.then_inc(xnb_ready, 1)
                if exists(b, u + 1):
                    k = (u + 1) % 2
                    pool.wait_ge(r_loaded[k], dma_nth(b, u + 1))
                    pool.tensor_tensor(xres[:, k], xres[:, k], rows4(beta_row), ALU.add).then_inc(xb_ready, 1)
                    pool.wait_ge(ve1_ready, nth(b, u + 1))
                    pool.tensor_tensor(rs1[:], ve1[:], minus_half[:, 0:TILES], ALU.pow).then_inc(rs1_ready, 1)
                if exists(b, u + 2):
                    k = u % 2
                    pool.wait_ge(xnb_ready, nth(b, u + 2))
                    if exists(b, u + 1):
                        pool.wait_ge(x1_sum, nth(b, u + 1))
                    pool.tensor_tensor(res1[:], xin[:, k], rows4(bout_row), ALU.add).then_inc(res1_ready, 1)
                    for p in (2, 3):
                        pool.wait_ge(qf_hi, nth(b, u + 2, p + 1, 4))
                        pool.tensor_tensor(flat(query_fs[1][:, 2 * p:2 * p + 2, :]), feat[:, p % 2, :],
                                           flat(query_fs[0][:, 2 * p:2 * p + 2, :]), ALU.subtract).then_inc(qf_lo_pool, 1)
                if exists(b, u + 1):
                    pool.wait_ge(zs_hi, nth(b, u + 1))
                    pool.tensor_tensor(zs[1][:], zq, zs[0][:].bitcast(F32), ALU.subtract).then_inc(zs_lo, 1)
                if exists(b, u + 2):
                    if exists(b, u + 1):
                        pool.wait_ge(zT_mm, nth(b, u + 1))
                    pool.wait_ge(xnb_ready, nth(b, u + 2))
                    hold()
                    for t in range(TILES):
                        last = pool.tensor_scalar(z[:, t, :], xin[:, k, t, :], stat[:, k, 4 + t:5 + t], 1.0,
                                                  ALU.mult, ALU.mult)
                    last.then_inc(zb_ready, 1)

            over_groups(pool, step_b)

        @block.scalar
        def _(act):
            for n, s in enumerate(WEIGHT_SLOTS):
                act.wait_ge(wT_mm, n + 1)
                if n in (2, 3):
                    act.copy(w1T[:, n - 2, :], pair_flat(s)).then_inc(w1_plain, 1)
                    continue
                for hi, src in weight_parts(n, 0):
                    last = act.copy(hi, src)
                last.then_inc(wT_hi, 1)
            act.wait_ge(w1_scaled, 1)
            act.copy(w1s[0][:], w1T).then_inc(wT_hi, 1)
            act.wait_ge(ld_proj, 16 * H)
            act.copy(projs[0], raw_proj).then_inc(proj_hi, 1)
            act.wait_ge(ld_stack, 12 * 16)
            act.copy(proj_stack[0:STACK], raw_stack[0:STACK]).then_inc(stack_hi, 1)
            act.wait_ge(ld_ffn, 16)
            act.activation(tern_a, raw_ffn.rearrange("p k u -> p (k u)"), ACT.Abs, accum_out=colsum).then_inc(w_abs, 1)

            def step_a(b, u):
                def high(w, t):
                    if exists(b, w):
                        act.wait_ge(kf_ready, nth(b, w, t + 1, 4))
                        if exists(b, w - 1):
                            act.wait_ge(kv_mm, nth(b, w - 1, t + 1, 4))
                        act.copy(key_fs[0][:, t, :], key_feat[t]).then_inc(kf_hi, 1)

                for t in range(TILES):
                    if exists(b, u + 1) and t == 0:
                        act.wait_ge(xnT_mm, nth(b, u + 1))
                        if exists(b, u):
                            act.wait_ge(v_mm, nth(b, u, 2, 2))
                        act.copy(xnT[0][:], pair(0)).then_inc(xnT_hi, 1)
                    if exists(b, u):
                        act.wait_ge(kf_mm, nth(b, u, t + 1, 4))
                        if exists(b, u - 1):
                            act.wait_ge(kf_lo, nth(b, u - 1, t + 1, 4))
                        act.activation(key_feat[t], pair_flat(1 + t % 2), ACT.Relu, scale=-1.0).then_inc(kf_neg, 1)
                    if t == 0:
                        high(u - 1, 3)
                    else:
                        high(u, t - 1)
                    if exists(b, u):
                        act.wait_ge(kf_neg, nth(b, u, t + 1, 4))
                        act.activation(key_feat[t], key_feat[t], ACT.Exp, scale=-1.0).then_inc(kf_exp, 1)
                    if exists(b, u + 1) and t == 2:
                        act.wait_ge(kT_mm, nth(b, u + 1))
                        if exists(b, u - 1):
                            act.wait_ge(kf_mm, nth(b, u - 1, 4, 4))
                        act.copy(keys[0][:, (u + 1) % 2], pair(0)).then_inc(kT_hi, 1)
                    if exists(b, u + 1) and t % 2 == 1:
                        i = t // 2
                        act.wait_ge(v_mm, nth(b, u + 1, i + 1, 2))
                        act.wait_ge(vals_ones, 2)
                        if exists(b, u - 1):
                            act.wait_ge(kv_mm, nth(b, u - 1, 2 * i + 2, 4))
                        act.copy(head_values(0, (u + 1) % 2, i), ps[:, 7, :].rearrange("p (h e) -> p h e", e=HD)).then_inc(v_hi, 1)

            over_groups(act, step_a)

            def step_b(b, u):
                def hidden_units(p):
                    act.wait_ge(w1_mm, nth(b, u, p + 1, 4))
                    if p >= 2:
                        act.wait_ge(h_lo, nth(b, u, p - 1, 3))
                    elif exists(b, u - 1):
                        if p == 0:
                            act.wait_ge(h_lo, nth(b, u - 1, 3, 3))
                        else:
                            act.wait_ge(h_lo_dve, nth(b, u - 1))
                    for a in range(2):
                        c = 2 * p + a
                        last = act.activation(hidden[:, p % 2, a * 512:(a + 1) * 512], ps[:, 2 * (p % 2) + a, :],
                                              ACT.Gelu, bias=b1_col[:, c:c + 1])
                    last.then_inc(gelu_done, 1)
                    act.wait_ge(gelu_done, nth(b, u, p + 1, 4))
                    if exists(b, u - 1):
                        act.wait_ge(w2_mm, nth(b, u - 1, 4, 4))
                    act.copy(hid[0][:, 2 * p:2 * p + 2, :].rearrange("p a c -> p (a c)"), hidden[:, p % 2]).then_inc(h_hi, 1)

                def query_exp(p):
                    act.wait_ge(qf_mm, nth(b, u + 2, p + 1, 4))
                    if p >= 2:
                        act.wait_ge(qf_lo_dve, nth(b, u + 2, p - 1, 2))
                    elif exists(b, u + 1):
                        act.wait_ge(qf_lo_pool, nth(b, u + 1, p + 1, 2))
                    q = feat[:, p % 2, :]
                    act.activation(q, pair_flat(2 + p % 2), ACT.Relu, scale=-1.0).then_inc(qf_neg, 1)
                    act.wait_ge(qf_neg, nth(b, u + 2, p + 1, 4))
                    act.activation(q, q, ACT.Exp, scale=-1.0).then_inc(qf_exp, 1)

                def query_high(p):
                    act.wait_ge(qf_ready, nth(b, u + 2, p + 1, 4))
                    if exists(b, u + 1):
                        act.wait_ge(at_mm, nth(b, u + 1, 2, 2))
                    act.copy(query_fs[0][:, 2 * p:2 * p + 2, :].rearrange("p a c -> p (a c)"), feat[:, p % 2, :]).then_inc(qf_hi, 1)

                if exists(b, u + 2):
                    act.wait_ge(qT_mm, nth(b, u + 2))
                    if exists(b, u + 1):
                        act.wait_ge(qf_mm, nth(b, u + 1, 4, 4))
                    act.copy(qT[0][:], pair(0)).then_inc(qT_hi, 1)
                if exists(b, u):
                    act.wait_ge(nT_mm, nth(b, u))
                    if exists(b, u - 1):
                        act.wait_ge(w1_mm, nth(b, u - 1, 4, 4))
                    act.copy(tT[0][:], pair(1)).then_inc(nT_hi, 1)
                    hidden_units(0)
                    hidden_units(1)
                if exists(b, u + 1):
                    act.wait_ge(aT_mm, nth(b, u + 1))
                    if exists(b, u + 2):
                        act.wait_ge(qT_mm, nth(b, u + 2))
                    act.copy(xnT[0][:], pair(2)).then_inc(aT_hi, 1)
                if exists(b, u):
                    hidden_units(2)
                    hidden_units(3)
                if exists(b, u + 2):
                    query_exp(0)
                    query_exp(1)
                    query_high(0)
                    query_high(1)
                    query_exp(2)
                    query_exp(3)
                    query_high(2)
                if exists(b, u + 3):
                    act.wait_ge(xT_mm, nth(b, u + 3))
                    if exists(b, u + 1):
                        act.wait_ge(wo_mm, nth(b, u + 1))
                    act.copy(xnT[0][:], pair(2)).then_inc(xT_hi, 1)
                if exists(b, u + 2):
                    query_high(3)
                if exists(b, u + 1):
                    act.wait_ge(zT_mm, nth(b, u + 1))
                    act.wait_ge(scales_ready, 1)
                    if exists(b, u):
                        act.wait_ge(zs_lo, nth(b, u))
                    for c in range(KD):
                        last = act.activation(zq[:, c, :], ps[:, 6 + c, :], ACT.Identity, bias=bz[:, c:c + 1], scale=gz[:, c:c + 1])
                    last.then_inc(zq_affine, 1)
                    act.wait_ge(zq_clipped, nth(b, u + 1))
                    if exists(b, u):
                        act.wait_ge(y_mm, nth(b, u))
                    act.copy(zs[0][:], zq).then_inc(zs_hi, 1)

            over_groups(act, step_b)

        @block.vector
        def _(dve):
            def hold():
                dve.sem_inc(dve_held, 1)

            dve.memset(raw_proj, 0.0).then_inc(proj_zero, 1)
            dve.memset(kv_mask[:], 0.0).then_inc(mask_zero, 1)
            dve.wait_ge(mask_zero, 1)
            mask_c = kv_mask[:].rearrange("p (c w) -> p c w", w=CW)
            dve.memset(mask_c[0:F, :, 0:VW], KV_SCALE).then_inc(mask_ready, 1)
            dve.memset(mask_c[F:P, :, VW:CW], KV_SCALE).then_inc(mask_ready, 1)
            dve.memset(vals[:, 0], 1.0).then_inc(vals_ones, 1)
            dve.memset(vals[:, 1], 0.0).then_inc(vals_ones, 1)

            done = 0
            for n, s in enumerate(WEIGHT_SLOTS):
                if n in (2, 3):
                    continue
                done += 1
                dve.wait_ge(wT_hi, done)
                for (lo, src), (hi, _) in zip(weight_parts(n, 1), weight_parts(n, 0)):
                    last = dve.tensor_tensor(lo, src, hi.bitcast(F32), ALU.subtract)
                last.then_inc(wT_lo, 1)
            dve.wait_ge(b1_mm, 1)
            dve.wait_ge(ld_cols, 16 * 5)
            dve.tensor_tensor(b1_col[:], ps[:, 4, 0:FC], b1_col[:], ALU.add).then_inc(b1_done, 1)
            for c in range(KD):
                last = dve.tensor_scalar(w1T[:, c, :], w1T[:, c, :], gamma_col[:, c:c + 1], None, ALU.mult)
            last.then_inc(w1_scaled, 1)
            dve.wait_ge(wT_hi, done + 1)
            dve.tensor_tensor(w1s[1][:], w1T, w1s[0][:].bitcast(F32), ALU.subtract).then_inc(wT_lo, 1)
            dve.wait_ge(proj_hi, 1)
            dve.tensor_tensor(projs[1], raw_proj, projs[0].bitcast(F32), ALU.subtract).then_inc(proj_lo, 1)
            dve.wait_ge(stack_hi, 1)
            low_rows = slice(STACK - PAIR_D, STACK)
            dve.tensor_tensor(proj_stack[low_rows], raw_stack[low_rows], proj_stack[low_rows], ALU.subtract).then_inc(stack_lo, 1)
            dve.wait_ge(ld_rows, 16 * 4)
            dve.tensor_tensor(b2_row[:], b2_row[:], beta_row[:], ALU.add).then_inc(w_chain, 1)
            dve.wait_ge(w_sum, 1)
            dve.tensor_scalar(w_mean, ps[:, 5, 0:1], 1.0 / (D * D), None, ALU.mult).then_inc(w_chain, 1)
            dve.wait_ge(w_chain, 2)
            dve.tensor_scalar(w_half, w_mean, EPS_FFN, 0.5, ALU.add, ALU.mult).then_inc(w_chain, 1)
            dve.tensor_scalar(y_scale, w_mean, 1.0 / QB, None, ALU.mult).then_inc(w_chain, 1)
            dve.wait_ge(w_chain, 3)
            dve.tensor_scalar(w_minus_half, w_half, -1.0, None, ALU.mult).then_inc(w_chain, 1)
            flat_ffn = raw_ffn.rearrange("p k u -> p (k u)")
            dve.tensor_scalar(tern_a, flat_ffn, w_half, None, ALU.is_gt).then_inc(w_chain, 1)
            dve.wait_ge(w_chain, 6)
            dve.tensor_scalar(tern_b, flat_ffn, w_minus_half, None, ALU.is_lt).then_inc(w_chain, 1)
            dve.wait_ge(w_chain, 7)
            dve.tensor_tensor(ternary[:].rearrange("p k u -> p (k u)"), tern_a, tern_b, ALU.subtract).then_inc(tern_done, 1)
            dve.memset(zmax, -3.0e38).then_inc(zinit, 1)
            dve.memset(zmin, 3.0e38).then_inc(zinit, 1)

            def moments(b, u, src, bn_t, mv_t, bn_s, mv_s):
                for t in range(TILES):
                    last = dve.bn_stats(bn_t[:, t, :], src[:, t, :])
                last.then_inc(bn_s, 1)
                dve.wait_ge(bn_s, nth(b, u))
                hold()
                for t in range(TILES):
                    last = dve.bn_aggr(mv_t[:, t, :], bn_t[:, t, :])
                last.then_inc(mv_s, 1)
                dve.wait_ge(mv_s, nth(b, u))

            def step_a(b, u):
                def extremes(best, op):
                    k = u % 2
                    dve.wait_ge(xn_ready, nth(b, u + 2))
                    if exists(b, u + 1):
                        dve.wait_ge(z_used, nth(b, u + 1))
                    else:
                        dve.wait_ge(zinit, 2)
                    for t in range(TILES):
                        last = dve.scalar_tensor_tensor(best[:, t, :], xin[:, k, t, :], stat[:, k, 4 + t:5 + t], best[:, t, :],
                                                        ALU.mult, op)
                    return last

                for t in range(TILES):
                    if exists(b, u + 1) and t == 0:
                        dve.wait_ge(xnT_hi, nth(b, u + 1))
                        dve.tensor_tensor(xnT[1][:], pair(0), xnT[0][:].bitcast(F32), ALU.subtract).then_inc(xnT_lo, 1)
                    if t == 3 and u % GPB == 0 and exists(b, u - 1):
                        dve.wait_ge(kv_mm, nth(b, u - 1, 4, 4))
                        dve.wait_ge(mask_ready, 2)
                        saved = kv_cols(b + u // GPB - 1)
                        dve.tensor_tensor(kv_new, ps[:, 6, 0:KVW], kv_mask[:], ALU.mult).then_inc(kv_new_done, 1)
                        dve.wait_ge(kv_new_done, b + u // GPB)
                        dve.tensor_copy(saved[:, 0:KVW], kv_new).then_inc(kv_hi, 1)
                        dve.wait_ge(kv_hi, b + u // GPB)
                        dve.tensor_tensor(saved[:, KVW:2 * KVW], kv_new, saved[:, 0:KVW], ALU.subtract).then_inc(kv_saved, 1)
                    if exists(b, u + 2) and t == 3:
                        extremes(zmax, ALU.max)
                    if exists(b, u):
                        dve.wait_ge(kf_exp, nth(b, u, t + 1, 4))
                        dve.scalar_tensor_tensor(key_feat[t], pair_flat(1 + t % 2), 0.0, key_feat[t],
                                                 ALU.max, ALU.add).then_inc(kf_ready, 1)
                    if exists(b, u + 2) and t == 3:
                        extremes(zmin, ALU.min).then_inc(z_used, 1)
                        dve.tensor_copy(stat_cols(b, u + 2), stat[:, u % 2, :]).then_inc(stat_saved, 1)
                    if exists(b, u + 1) and t == 2:
                        dve.wait_ge(kT_hi, nth(b, u + 1))
                        dve.tensor_tensor(keys[1][:, (u + 1) % 2], pair(0), keys[0][:, (u + 1) % 2].bitcast(F32),
                                          ALU.subtract).then_inc(kT_lo, 1)
                    if exists(b, u + 1) and t % 2 == 1:
                        i, k = t // 2, (u + 1) % 2
                        dve.wait_ge(v_hi, nth(b, u + 1, i + 1, 2))
                        dve.tensor_tensor(head_values(1, k, i), ps[:, 7, :].rearrange("p (h e) -> p h e", e=HD), head_values(0, k, i),
                                          ALU.subtract).then_inc(v_ready, 1)
                    if exists(b, u + 3) and t == 1:
                        k = (u + 3) % 2
                        dve.wait_ge(x_loaded[k], dma_nth(b, u + 3))
                        moments(b, u + 3, xin[:, k], bn, mv, bn_done, mv_done)
                        if exists(b, u + 2):
                            dve.wait_ge(std_ready, nth(b, u + 2))
                        if exists(b, u + 1):
                            dve.wait_ge(stat_saved, nth(b, u + 1))
                        dve.tensor_scalar(stat[:, k, 8:12], mv[:, :, 0], -1.0, None, ALU.mult)
                        dve.tensor_scalar(pw[:, 0:TILES], mv[:, :, 1], EPS_LN, None, ALU.add).then_inc(ve_done, 1)
                        dve.wait_ge(ve_done, nth(b, u + 3))
                        dve.reciprocal(inv[:], pw[:, 0:TILES]).then_inc(inv_done, 1)
                        dve.wait_ge(inv_done, nth(b, u + 3))
                        dve.tensor_tensor(inv[:], inv[:], mv[:, :, 1], ALU.mult).then_inc(ratio_done, 1)
                        dve.wait_ge(ratio_done, nth(b, u + 3))
                        dve.tensor_scalar(pw[:, TILES:8], inv[:], EPS_FFN_LN, None, ALU.add).then_inc(pw_ready, 1)

            over_groups(dve, step_a)

            dve.wait_ge(z_used, GROUPS)
            zf = [zmax.rearrange("p t d -> p (t d)"), zmin.rearrange("p t d -> p (t d)")]
            for step, width in enumerate((2 * D, D)):
                for a, op in zip(zf, (ALU.max, ALU.min)):
                    last = dve.tensor_tensor(a[:, 0:width], a[:, 0:width], a[:, width:2 * width], op)
                    last.then_inc(zm_part if step == 0 else zmT_in, 1)
                dve.wait_ge(zm_part, 2)
            dve.wait_ge(zmT_mm, 1)
            dve.tensor_reduce(zext[:, 0:2], ps[:, 0, 0:256].rearrange("p (k n) -> p k n", k=2), AX_X, ALU.max)
            dve.tensor_reduce(zext[:, 2:4], ps[:, 0, 256:512].rearrange("p (k n) -> p k n", k=2), AX_X, ALU.min).then_inc(zext_done, 1)
            dve.wait_ge(zext_done, 1)
            for i in range(2):
                last = dve.tensor_tensor(zext[:, 2 * i:2 * i + 2], zext[:, 2 * i:2 * i + 2], lng_col[:], ALU.mult)
            last.then_inc(g_chain, 1)
            dve.wait_ge(g_chain, 1)
            for i in range(2):
                last = dve.tensor_tensor(zext[:, 2 * i:2 * i + 2], zext[:, 2 * i:2 * i + 2], lnb_col[:], ALU.add)
            last.then_inc(g_chain, 1)
            dve.wait_ge(g_chain, 2)
            dve.tensor_scalar(zabs, zext, -1.0, None, ALU.mult).then_inc(g_chain, 1)
            dve.wait_ge(g_chain, 3)
            dve.tensor_tensor(zabs, zabs, zext, ALU.max).then_inc(g_chain, 1)
            dve.wait_ge(g_chain, 4)
            dve.tensor_reduce(zpart, zabs, AX_X, ALU.max).then_inc(zm_done, 1)
            dve.wait_ge(zpart_mm, 1)
            dve.tensor_reduce(small[0:1, 21:22], ps[0:1, 2, 0:P], AX_X, ALU.max).then_inc(g_one, 1)
            dve.wait_ge(g_all, 1)
            dve.tensor_copy(gmax, ps[:, 4, 0:1]).then_inc(g_chain, 1)
            dve.wait_ge(g_chain, 5)
            dve.reciprocal(qscale, gmax).then_inc(g_chain, 1)
            dve.tensor_tensor(y_scale, y_scale, gmax, ALU.mult).then_inc(scales_y, 1)
            dve.wait_ge(g_chain, 6)
            dve.tensor_scalar(gz, lng_col[:], qscale, QB, ALU.mult, ALU.mult)
            dve.tensor_scalar(bz, lnb_col[:], qscale, QB, ALU.mult, ALU.mult).then_inc(scales_ready, 1)

            def flat(a):
                return a.rearrange("p t d -> p (t d)")

            def step_b(b, u):
                def query_sum(p):
                    dve.wait_ge(qf_exp, nth(b, u + 2, p + 1, 4))
                    dve.scalar_tensor_tensor(feat[:, p % 2, :], pair_flat(2 + p % 2), 0.0, feat[:, p % 2, :],
                                             ALU.max, ALU.add).then_inc(qf_ready, 1)

                def query_low(p):
                    dve.wait_ge(qf_hi, nth(b, u + 2, p + 1, 4))
                    dve.tensor_tensor(flat(query_fs[1][:, 2 * p:2 * p + 2, :]), feat[:, p % 2, :],
                                      flat(query_fs[0][:, 2 * p:2 * p + 2, :]), ALU.subtract).then_inc(qf_lo_dve, 1)

                if exists(b, u - 1):
                    dve.wait_ge(w2_mm, nth(b, u - 1, 4, 4))
                    dve.wait_ge(res2_ready, nth(b, u - 1))
                    if exists(b, u - 2):
                        dve.wait_ge(out_ready, nth(b, u - 2))
                    dve.tensor_tensor(flat(x2), pair_flat(1), flat(res2), ALU.add).then_inc(x2_sum, 1)
                    dve.wait_ge(x2_sum, nth(b, u - 1))
                    moments(b, u - 1, x2, bn2, mv2, bn2_done, mv2_done)
                    if exists(b, u - 2):
                        dve.wait_ge(rs2_ready, nth(b, u - 2))
                    dve.tensor_scalar(ve2[:], mv2[:, :, 1], EPS_LN, None, ALU.add).then_inc(ve2_ready, 1)
                if exists(b, u + 2):
                    dve.wait_ge(qT_hi, nth(b, u + 2))
                    dve.tensor_tensor(qT[1][:], pair(0), qT[0][:], ALU.subtract).then_inc(qT_lo, 1)
                if exists(b, u):
                    dve.wait_ge(nT_hi, nth(b, u))
                    dve.tensor_tensor(tT[1][:], pair(1), tT[0][:].bitcast(F32), ALU.subtract).then_inc(nT_lo, 1)
                if exists(b, u + 1):
                    for a in range(2):
                        dve.wait_ge(at_mm, nth(b, u + 1, a + 1, 2))
                        if exists(b, u):
                            dve.wait_ge(aT_mm, nth(b, u))
                            dve.wait_ge(zs_lo, nth(b, u))
                        sums = ps[:, 4 + 2 * a:6 + 2 * a, 0:KVW].rearrange("p t (h e) -> p t h e", e=VW)
                        r = rden[:, 2 * a:2 * a + 2, :]
                        dve.tensor_scalar(r, sums[:, :, :, HD], EPS_ATTN * KV_SCALE, None, ALU.add).then_inc(den_done, 1)
                        dve.wait_ge(den_done, nth(b, u + 1, a + 1, 2))
                        dve.reciprocal(r, r).then_inc(rden_done, 1)
                        dve.wait_ge(rden_done, nth(b, u + 1, a + 1, 2))
                        dve.tensor_tensor(attn[:, 2 * a:2 * a + 2, :].rearrange("p t (h e) -> p t h e", e=HD),
                                          sums[:, :, :, 0:HD], r.unsqueeze(3).broadcast_to([P, 2, H, HD]),
                                          ALU.mult).then_inc(at_ready, 1)
                if exists(b, u - 1):
                    k = (u - 1) % 2
                    for t in range(TILES):
                        last = dve.scalar_tensor_tensor(x2[:, t, :], x2[:, t, :], mv2[:, t, 0:1], gamma_row[:],
                                                        ALU.subtract, ALU.mult)
                    last.then_inc(x2_scaled, 1)
                    dve.wait_ge(x2_scaled, nth(b, u - 1))
                    dve.wait_ge(rs2_ready, nth(b, u - 1))
                    dve.wait_ge(acc_ready, nth(b, u - 1))
                    for t in range(TILES):
                        last = dve.scalar_tensor_tensor(xres[:, k, t, :], x2[:, t, :], rs2[:, t:t + 1], xres[:, k, t, :],
                                                        ALU.mult, ALU.add)
                    last.then_inc(out_ready, 1)
                if exists(b, u + 3):
                    k = (u + 3) % 2
                    if exists(b, u + 1):
                        dve.wait_ge(zb_ready, nth(b, u + 1))
                    dve.tensor_copy(stat[:, k, :], stat_cols(b, u + 3)).then_inc(stat_got, 1)
                if exists(b, u + 1):
                    dve.wait_ge(aT_hi, nth(b, u + 1))
                    dve.tensor_tensor(xnT[1][:], pair(2), xnT[0][:].bitcast(F32), ALU.subtract).then_inc(aT_lo, 1)
                if exists(b, u):
                    dve.wait_ge(h_hi, nth(b, u, 4, 4))
                    dve.tensor_tensor(flat(hid[1][:, 6:8, :]), hidden[:, 1], flat(hid[0][:, 6:8, :]).bitcast(F32),
                                      ALU.subtract).then_inc(h_lo_dve, 1)
                if exists(b, u + 1):
                    dve.wait_ge(wo_mm, nth(b, u + 1))
                    dve.wait_ge(res1_ready, nth(b, u + 1))
                    if exists(b, u):
                        dve.wait_ge(nT_mm, nth(b, u))
                        dve.wait_ge(res2_ready, nth(b, u))
                    dve.tensor_tensor(flat(n1), pair_flat(3), flat(res1), ALU.add).then_inc(x1_sum, 1)
                    dve.wait_ge(x1_sum, nth(b, u + 1))
                    moments(b, u + 1, n1, bn1, mv1, bn1_done, mv1_done)
                    if exists(b, u):
                        dve.wait_ge(rs1_ready, nth(b, u))
                    dve.tensor_scalar(ve1[:], mv1[:, :, 1], EPS_LN, None, ALU.add).then_inc(ve1_ready, 1)
                if exists(b, u + 2):
                    query_sum(0)
                    query_sum(1)
                    query_low(0)
                if exists(b, u):
                    k = u % 2
                    dve.wait_ge(y_mm, nth(b, u))
                    dve.wait_ge(xb_ready, nth(b, u))
                    dve.scalar_tensor_tensor(flat(xres[:, k]), pair_flat(0), y_scale, flat(xres[:, k]),
                                             ALU.mult, ALU.add).then_inc(acc_ready, 1)
                if exists(b, u + 2):
                    query_low(1)
                    query_sum(2)
                if exists(b, u + 1):
                    dve.wait_ge(rs1_ready, nth(b, u + 1))
                    hold()
                    for t in range(TILES):
                        last = dve.tensor_scalar(n1[:, t, :], n1[:, t, :], mv1[:, t, 0:1], rs1[:, t:t + 1], ALU.subtract, ALU.mult)
                    last.then_inc(n1_ready, 1)
                if exists(b, u + 2):
                    query_sum(3)
                    if (u + 2) % GPB == 0:
                        dve.wait_ge(kv_saved, B)
                        if exists(b, u + 1):
                            dve.wait_ge(at_mm, nth(b, u + 1, 2, 2))
                        dve.tensor_copy(kv_cur, kv_cols(b + (u + 2) // GPB)).then_inc(kv_ready, 1)
                if exists(b, u + 3):
                    dve.wait_ge(xT_hi, nth(b, u + 3))
                    dve.tensor_tensor(xnT[1][:], pair(2), xnT[0][:].bitcast(F32), ALU.subtract).then_inc(xT_lo, 1)
                if exists(b, u + 1):
                    dve.wait_ge(zq_affine, nth(b, u + 1))
                    dve.tensor_scalar(zq, zq, CLIP, -CLIP, ALU.min, ALU.max).then_inc(zq_clipped, 1)

            over_groups(dve, step_b)

        @block.tensor
        def _(pe):
            pe.wait_ge(consts_set, 4)
            done = 0
            for n, s in enumerate(WEIGHT_SLOTS):
                if n == 0:
                    pe.wait_ge(ld_qkv, 32)
                if n == 2:
                    pe.wait_ge(ld_w1, 16)
                if n == 4:
                    pe.wait_ge(ld_w2, 16)
                    pe.wait_ge(wT_lo, 2)
                for col, src in weight_blocks(n):
                    last = pe.transpose(pair_flat(s)[:, col:col + P], src, ident[:])
                last.then_inc(wT_mm, 1)
            pe.wait_ge(w1_plain, 2)
            pe.wait_ge(ld_cols, 16 * 5)
            for c in range(FC):
                for d in range(KD):
                    last = pe.matmul(ps[:, 4, c:c + 1], w1T[:, d, c * P:(c + 1) * P], beta_col[:, d:d + 1],
                                     start=(c == 0 and d == 0), stop=(c == FC - 1 and d == KD - 1), skip_group_check=True)
            last.then_inc(b1_mm, 1)
            pe.wait_ge(w_abs, 1)
            pe.matmul(ps[:, 5, 0:1], ones[:], colsum, start=True, stop=True).then_inc(w_sum, 1)
            pe.wait_ge(wT_lo, 5)
            pe.wait_ge(proj_lo, 1)
            pe.wait_ge(b1_done, 1)
            pe.wait_ge(tern_done, 1)

            def transposes(dst, src):
                for c in range(KD):
                    for t in range(TILES):
                        last = pe.transpose(dst[:, c, tile_cols(t)], src[:, t, tile_cols(c)], ident[:])
                return last

            def step_a(b, u):
                def key_features(t):
                    if t == 0:
                        pe.wait_ge(kT_lo, nth(b, u))
                    if t >= 2:
                        pe.wait_ge(kf_ready, nth(b, u, t - 1, 4))
                    elif exists(b, u - 1):
                        pe.wait_ge(kf_ready, nth(b, u - 1, t + 3, 4))
                    for hg in range(KD):
                        last = three_passes(pe, ps[:, 2 + 2 * (t % 2) + hg, :],
                                            lambda c: tuple(part[:, u % 2, c, tile_cols(t)] for part in keys),
                                            columns(projs, slice(None)), [hg])
                    last.then_inc(kf_mm, 1)

                def values(i):
                    pe.wait_ge(xnT_lo, nth(b, u + 1))
                    if i == 1:
                        pe.wait_ge(v_ready, nth(b, u + 1, 1, 2))
                    elif exists(b, u):
                        pe.wait_ge(v_ready, nth(b, u, 2, 2))
                    for t in range(2):
                        last = three_passes(pe, ps[:, 7, t * D:(t + 1) * D], columns(xnT, tile_cols(2 * i + t)),
                                            columns(wv, slice(None)), range(KD))
                    last.then_inc(v_mm, 1)

                def sums(w, i):
                    pe.wait_ge(kf_lo, nth(b, w, i + 1, 4))
                    if i % 2 == 0:
                        pe.wait_ge(v_ready, nth(b, w, i // 2 + 1, 2))
                    if i == 0 and w % GPB == 0 and exists(b, w - 1):
                        pe.wait_ge(kv_new_done, b + w // GPB)
                    for c in range(HC):
                        first = w % GPB == 0 and i == 0 and c == 0
                        end = w % GPB == GPB - 1 and i == TILES - 1 and c == HC - 1
                        for n, (f, v) in enumerate(PASSES):
                            last = pe.matmul(ps[:, 6, c * CW:(c + 1) * CW], key_fs[f][:, i, c * P:(c + 1) * P],
                                             vals[:, v, w % 2, i, c * CW:(c + 1) * CW], start=first and n == 0,
                                             stop=end and n == len(PASSES) - 1, skip_group_check=True)
                    last.then_inc(kv_mm, 1)

                for t in range(TILES):
                    if exists(b, u + 1) and t == 0:
                        pe.wait_ge(xn_ready, nth(b, u + 1))
                        if exists(b, u):
                            pe.wait_ge(kT_lo, nth(b, u))
                        transposes(pair(0), xin[:, (u + 1) % 2]).then_inc(xnT_mm, 1)
                    if exists(b, u):
                        key_features(t)
                    if exists(b, u + 1) and t == 2:
                        pe.wait_ge(xnT_lo, nth(b, u + 1))
                        for m in range(KD):
                            last = three_passes(pe, ps[:, m, :], columns(wk, tile_cols(m)), columns(xnT, slice(None)), range(KD))
                        last.then_inc(kT_mm, 1)
                    if exists(b, u + 1) and t % 2 == 1:
                        values(t // 2)
                    w, i = (u - 1, t + 1) if t < 3 else (u, 0)
                    if exists(b, w):
                        sums(w, i)

            over_groups(pe, step_a)

            pe.wait_ge(zmT_in, 2)
            pe.wait_ge(kT_lo, GROUPS)
            for n, a in enumerate((zmax, zmin)):
                for c in range(KD):
                    col = (n * KD + c) * P
                    last = pe.transpose(ps[:, 0, col:col + P], a.rearrange("p t d -> p (t d)")[:, c * P:(c + 1) * P], ident[:])
            last.then_inc(zmT_mm, 1)
            pe.wait_ge(zm_done, 1)
            pe.transpose(ps[0:1, 2, 0:P], zpart, ident[:]).then_inc(zpart_mm, 1)
            pe.wait_ge(g_one, 1)
            pe.matmul(ps[:, 4, 0:1], ones[0:1, :], small[0:1, 21:22], start=True, stop=True).then_inc(g_all, 1)
            pe.wait_ge(scales_ready, 1)
            pe.wait_ge(stack_lo, 1)
            pe.wait_ge(kv_saved, B)

            def step_b(b, u):
                def query_features(p):
                    if p == 0:
                        pe.wait_ge(q_stacked, nth(b, u + 2, 192, 192))
                        if exists(b, u + 1):
                            pe.wait_ge(aT_lo, nth(b, u + 1))
                    elif p == 1:
                        if exists(b, u + 1):
                            pe.wait_ge(x1_sum, nth(b, u + 1))
                    else:
                        pe.wait_ge(qf_ready, nth(b, u + 2, p - 1, 4))
                    for a in range(2):
                        c = 2 * p + a
                        last = pe.matmul(ps[:, 4 + 2 * (p % 2) + a, :], proj_stack[0:STACK, c, :], q_stack[0:STACK, c, :],
                                         start=True, stop=True)
                    last.then_inc(qf_mm, 1)

                def hidden_units(p):
                    if p == 0:
                        pe.wait_ge(nT_lo, nth(b, u))
                        if exists(b, u + 2):
                            pe.wait_ge(qT_lo, nth(b, u + 2))
                    if p >= 2:
                        pe.wait_ge(gelu_done, nth(b, u, p - 1, 4))
                    for a in range(2):
                        c = 2 * p + a
                        last = three_passes(pe, ps[:, 2 * (p % 2) + a, :], columns(w1s, tile_cols(c)),
                                            columns(tT, slice(None)), range(KD))
                    last.then_inc(w1_mm, 1)

                def out_tile(t):
                    if t == 0:
                        pe.wait_ge(h_lo, nth(b, u, 3, 3))
                        pe.wait_ge(h_lo_dve, nth(b, u))
                    three_passes(pe, pair_flat(1)[:, t * D:(t + 1) * D], columns(hid, tile_cols(t)),
                                 columns(w2s, slice(None)), range(FC)).then_inc(w2_mm, 1)

                if exists(b, u):
                    pe.wait_ge(n1_ready, nth(b, u))
                    if exists(b, u - 1):
                        pe.wait_ge(x2_sum, nth(b, u - 1))
                    transposes(pair(1), n1).then_inc(nT_mm, 1)
                if exists(b, u + 1):
                    pe.wait_ge(qf_hi, nth(b, u + 1, 4, 4))
                    pe.wait_ge(qf_lo_dve, nth(b, u + 1, 2, 2))
                    pe.wait_ge(qf_lo_pool, nth(b, u + 1, 2, 2))
                    pe.wait_ge(kv_ready, b + (u + 1) // GPB + 1)
                    if exists(b, u + 2):
                        pe.wait_ge(xT_lo, nth(b, u + 2))
                    if exists(b, u):
                        pe.wait_ge(zq_affine, nth(b, u))
                    for t in range(TILES):
                        for c in range(HC):
                            for n, (f, v) in enumerate(PASSES):
                                last = pe.matmul(ps[:, 4 + t, c * CW:(c + 1) * CW], query_fs[f][:, c, tile_cols(t)],
                                                 kv_cur[:, v * KVW + c * CW:v * KVW + (c + 1) * CW], start=(c == 0 and n == 0),
                                                 stop=(c == HC - 1 and n == len(PASSES) - 1), skip_group_check=True)
                        if t % 2:
                            last.then_inc(at_mm, 1)
                if exists(b, u):
                    hidden_units(0)
                    hidden_units(1)
                if exists(b, u + 1):
                    pe.wait_ge(at_ready, nth(b, u + 1, 2, 2))
                    transposes(pair(2), attn).then_inc(aT_mm, 1)
                if exists(b, u):
                    hidden_units(2)
                    hidden_units(3)
                if exists(b, u + 2):
                    query_features(0)
                if exists(b, u + 1):
                    pe.wait_ge(aT_lo, nth(b, u + 1))
                    for t in range(TILES):
                        last = three_passes(pe, pair_flat(3)[:, t * D:(t + 1) * D], columns(xnT, tile_cols(t)),
                                            columns(wo, slice(None)), range(KD))
                    last.then_inc(wo_mm, 1)
                if exists(b, u):
                    pe.wait_ge(zs_lo, nth(b, u))
                    pe.wait_ge(gelu_done, nth(b, u, 3, 4))
                    for t in range(TILES):
                        steps = [(c, part) for c in range(KD) for part in zs]
                        for n, (c, part) in enumerate(steps):
                            last = pe.matmul(pair_flat(0)[:, t * D:(t + 1) * D], part[:, c, tile_cols(t)], ternary[:, c, :],
                                             start=(n == 0), stop=(n == len(steps) - 1))
                    last.then_inc(y_mm, 1)
                for p in range(1, 4):
                    if exists(b, u + 2):
                        query_features(p)
                    if exists(b, u):
                        out_tile(p - 1)
                if exists(b, u + 3):
                    pe.wait_ge(xnb_ready, nth(b, u + 3))
                    if exists(b, u + 2):
                        pe.wait_ge(qf_ready, nth(b, u + 2, 3, 4))
                    transposes(pair(2), xin[:, (u + 3) % 2]).then_inc(xT_mm, 1)
                if exists(b, u + 1):
                    pe.wait_ge(zb_ready, nth(b, u + 1))
                    if exists(b, u + 2):
                        pe.wait_ge(qf_ready, nth(b, u + 2, 4, 4))
                    else:
                        pe.wait_ge(x1_sum, nth(b, u + 1))
                    transposes(pair(3), z).then_inc(zT_mm, 1)
                if exists(b, u):
                    out_tile(3)
                if exists(b, u + 3):
                    pe.wait_ge(xT_lo, nth(b, u + 3))
                    if exists(b, u):
                        pe.wait_ge(acc_ready, nth(b, u))
                    for m in range(KD):
                        last = three_passes(pe, ps[:, m, :], columns(wq, tile_cols(m)), columns(xnT, slice(None)), range(KD))
                    last.then_inc(qT_mm, 1)

            over_groups(pe, step_b)


_INS = ['L0_attn_x', 'L0_attn_proj', 'L0_attn_w_qkv', 'L0_attn_w_out', 'L0_attn_b_out', 'L0_attn_gamma', 'L0_attn_beta',
        'L0_attn_w1', 'L0_attn_b1', 'L0_attn_w2', 'L0_attn_b2', 'L0_ffn_weight', 'L0_ffn_ln_gamma', 'L0_ffn_ln_beta']
_OUTS = [((B, N, D), 'float32')]


def kernel(**inputs):
    import numpy as _np
    import concourse.bacc as _bacc
    from concourse import mybir as _mybir
    from concourse.bass_utils import run_bass_kernel_spmd as _run

    nc = _bacc.Bacc("TRN2", target_bir_lowering=False, num_devices=1)
    arrays, args = {}, []
    for name in _INS:
        a = _np.ascontiguousarray(inputs[name])
        arrays[f"in_{name}_dram"] = a
        args.append(nc.dram_tensor(f"in_{name}_dram", a.shape, _mybir.dt.from_np(a.dtype), kind="ExternalInput").ap())
    for i, (shape, dtype) in enumerate(_OUTS):
        dt = _mybir.dt.from_np(_np.dtype(dtype))
        args.append(nc.dram_tensor(f"out_{i}_dram", shape, dt, kind="ExternalOutput").ap())
    linear_attention_block(nc, *args)
    r = _run(nc, [arrays], core_ids=[0])
    got = tuple(r.results[0][f"out_{i}_dram"] for i in range(len(_OUTS)))
    return got[0]
```

```python
from contextlib import ExitStack

import concourse.bass as bass
from concourse import mybir

F32 = mybir.dt.float32
F32R = mybir.dt.float32r
F16 = mybir.dt.float16
ALU = mybir.AluOpType
ACT = mybir.ActivationFunctionType
AX_X = mybir.AxisListType.X

P = 128
B, N, D = 8, 2048, 256
H, HD, F = 16, 16, 64
FF = 4 * D
TILES = 4
GT = TILES * P
GPB = N // GT
GROUPS = B * GPB
KD = D // P
HC = H * F // P
FC = FF // P
VW = HD + 1
CW = 2 * VW
KVW = HC * CW
PAIR = 2 * 512

EPS_LN = 1e-5
EPS_ATTN = 1e-8
EPS_FFN_LN = 1e-3
EPS_FFN = 1e-5
QB = 128.0
CLIP = QB - EPS_FFN
PASSES = (0, 0), (0, 1), (1, 0)
PAIR_D = 2 * HD
STACK = len(PASSES) * PAIR_D
W_SCALE = 2.0 ** 6
KV_SCALE = 1.0 / N


def nth(b, u, j=1, per=1):
    return b * (GPB * per) + (per * u + j)


def exists(b, u):
    return not isinstance(b, int) or 0 <= GPB * b + u < GROUPS


def dma_nth(b, u):
    return b * (16 * GPB // 2) + 16 * ((u - u % 2) // 2 + 1)


def over_groups(eng, step, lead, last=GPB):
    for u in range(-lead, GPB):
        step(0, u)
    with eng.Fori(1, B - 1) as b:
        for u in range(GPB):
            step(b, u)
    for u in range(last):
        step(B - 1, u)


def linear_attention_block(nc, x, proj, w_qkv, w_out, b_out, gamma, beta, w1, b1, w2, b2,
                           ffn_weight, ln_gamma, ln_beta, out):
    x_rows = x.rearrange("b n d -> (b n) d").rearrange("(g p t) d -> g p t d", p=P, t=TILES)
    out_rows = out.rearrange("b n d -> (b n) d").rearrange("(g p t) d -> g p t d", p=P, t=TILES)

    with ExitStack() as ctx:
        def sb(name, shape, dt=F32):
            return ctx.enter_context(nc.sbuf_tensor(name, shape, dt))

        def sem(name):
            return ctx.enter_context(nc.semaphore(name))

        ps = ctx.enter_context(nc.psum_tensor("ps", [P, 8, 512], F32))

        def pair(s):
            return ps[:, 2 * s:2 * s + 2, :]

        def pair_flat(s):
            return pair(s).rearrange("p a b -> p (a b)")

        ident = sb("ident", [P, P])
        ones = sb("ones", [P, P])
        minus_half = sb("minus_half", [P, 8])

        def split(name, shape, dt=F32R):
            return sb(name + "_hi", shape, dt), sb(name + "_lo", shape, dt)

        wq = split("wq", [P, KD, D])
        wkv = split("wkv", [P, KD, 2 * D])
        wk, wv = (tuple(w[:, :, i * D:(i + 1) * D] for w in wkv) for i in range(2))
        wo = split("wo", [P, KD, D], F16)
        w1s = split("w1s", [P, KD, FF], F16)
        w2s = split("w2s", [P, FC, D])
        proj_stack = sb("proj_stack", [P, HC, P], F16)
        ternary = sb("ternary", [P, KD, D], F32R)
        gamma_row, beta_row, bout_row, b2_row = (sb(n, [P, D]) for n in ("gamma_row", "beta_row", "bout_row", "b2_row"))
        gamma_col, beta_col, lng_col, lnb_col = (sb(n, [P, KD]) for n in ("gamma_col", "beta_col", "lng_col", "lnb_col"))
        b1_col = sb("b1_col", [P, FC])
        small = sb("small", [P, 32])
        w_mean, w_half, w_minus_half, gmax, qscale, y_scale, colsum = (small[:, i:i + 1] for i in range(7))
        gz, bz = small[:, 8:10], small[:, 10:12]
        zext, zabs, zpart = small[:, 12:16], small[:, 16:20], small[:, 20:21]

        q_parts = nc.dram_tensor("q_parts", [GROUPS, 2, KD * P, GT], F16).ap()

        xin = sb("xin", [P, 2, TILES, D])
        z = sb("z", [P, TILES, D])
        xnT = split("xnT", [P, KD, GT])
        feat = sb("feat", [P, 2, PAIR])
        fs = sb("fs_hi", [P, HC * 512], F16), sb("fs_lo", [P, HC * 512], F16)
        hf = sb("hf", [P, 2 * TILES * KVW])
        hid = split("hid", [P, FC, GT])
        xres = sb("xres", [P, 2, TILES, D])
        stats = sb("stats", [P, GROUPS * 12])
        stat = sb("stat", [P, 2, 12])
        kv_all = sb("kv_all", [P, B * 2 * KVW], F16)
        kv_buf = sb("kv_buf", [P, KVW])
        kv_mask, kv_cur = kv_buf, kv_buf[:].bitcast(F16)
        q_stack = sb("q_stack", [P, HC, GT], F16)
        qT = sb("qT_hi", [P, KD, GT], F16), sb("qT_lo", [P, KD, GT], F16)
        attn = sb("attn", [P, TILES, D])
        tT = split("tT", [P, KD, GT])
        n1 = sb("n1", [P, TILES, D])
        res1 = sb("res1", [P, TILES, D])
        res2 = sb("res2", [P, TILES, D])
        x2 = sb("x2", [P, TILES, D])
        zq = z.rearrange("p t d -> p (t d)").rearrange("p (k t) -> p k t", k=KD)
        zs = wkv
        bn = sb("bn", [P, TILES, 6])
        mv = sb("mv", [P, TILES, 2])
        pw = sb("pw", [P, 8])
        inv = sb("inv", [P, TILES])
        mv1, mv2 = sb("mv1", [P, TILES, 2]), sb("mv2", [P, TILES, 2])
        bn1, bn2 = sb("bn1", [P, TILES, 6]), sb("bn2", [P, TILES, 6])
        ve1, ve2 = sb("ve1", [P, TILES]), sb("ve2", [P, TILES])
        rs1, rs2 = sb("rs1", [P, TILES]), sb("rs2", [P, TILES])
        rden = sb("rden", [P, TILES, H])

        xnTs = (tuple(part[:] for part in xnT), tuple(part[:] for part in tT))
        kT = attn.rearrange("p t d -> p (t d)").bitcast(F16).rearrange("p (i k t) -> p i k t", i=2, k=KD)
        k_stack = [part.rearrange("p c t -> p (c t)").bitcast(F16).rearrange("p (i c t) -> p i c t", i=2, c=HC)[:, i]
                   for part in hid for i in range(2)]
        aT, nT = qT, split("nT", [P, KD, GT], F16)
        at_parts, n1_parts = split("at_parts", [P, KD * GT], F16), split("n1_parts", [P, KD * GT], F16)
        key_feat = [feat[:, 0, :], feat[:, 1, :], n1.rearrange("p t d -> p (t d)"), res1.rearrange("p t d -> p (t d)")]
        key_fs = [f.rearrange("p (t c) -> p t c", t=TILES) for f in fs]
        query_fs = [f.rearrange("p (c t) -> p c t", c=HC) for f in fs]
        vals = hf[:].bitcast(F16).rearrange("p (i k t c) -> p i k t c", i=2, k=2, t=TILES)
        query_feat = [attn.rearrange("p t d -> p (t d)"), x2.rearrange("p t d -> p (t d)"), feat[:, 0, :], feat[:, 1, :]]
        QUERY_PAIRS = (2, 0, 3, 2)
        raw_stack = x2.rearrange("p t d -> p (t d)").rearrange("p (c f) -> p c f", c=HC)
        kv_new = res2.rearrange("p t d -> p (t d)")[:, 0:KVW]
        hidden = hf[:, 0:2 * PAIR].rearrange("p (k c) -> p k c", k=2)
        zmax, zmin = xres[:, 0], xres[:, 1]
        raw_w1 = feat.rearrange("p a c -> p (a c)").rearrange("p (r d) -> p r d", d=D)
        raw_w2 = fs[0][:].bitcast(F32).rearrange("p (r f) -> p r f", f=FF)
        raw_qkv = q_stack.rearrange("p c t -> p (c t)").bitcast(F32)[:, 0:6 * D].rearrange("p (r d) -> p r d", d=D)
        raw_out = qT[0].rearrange("p k t -> p (k t)").bitcast(F32).rearrange("p (r d) -> p r d", d=D)
        raw_ffn = n1[:, 0:2, :]
        w1T = fs[1][:].bitcast(F32).rearrange("p (k c) -> p k c", k=KD)
        tern_a, tern_b = res1.rearrange("p t d -> p (t d)")[:, 0:KD * D], res2.rearrange("p t d -> p (t d)")[:, 0:KD * D]

        consts_set, proj_zero, mask_zero, mask_ready = sem("consts_set"), sem("proj_zero"), sem("mask_zero"), sem("mask_ready")
        ld_qkv, ld_w1, ld_w2, ld_ffn, ld_proj, ld_cols, ld_rows = (
            sem(n) for n in ("ld_qkv", "ld_w1", "ld_w2", "ld_ffn", "ld_proj", "ld_cols", "ld_rows"))
        wT_mm, wT_hi, wT_lo = sem("wT_mm"), sem("wT_hi"), sem("wT_lo")
        w1_plain, b1_mm, b1_done = sem("w1_plain"), sem("b1_mm"), sem("b1_done")
        w_abs, w_sum, w_chain, tern_done = sem("w_abs"), sem("w_sum"), sem("w_chain"), sem("tern_done")
        stack_hi, stack_lo = sem("stack_hi"), sem("stack_lo")
        vals_ones, zinit = sem("vals_ones"), sem("zinit")

        x_loaded = [sem("x_loaded0"), sem("x_loaded1")]
        bn_done, mv_done, ve_done, inv_done, ratio_done, pw_ready = (
            sem(n) for n in ("bn_done", "mv_done", "ve_done", "inv_done", "ratio_done", "pw_ready"))
        std_ready, xn_ready, z_ready, zmax_done, z_used, stat_saved = (
            sem(n) for n in ("std_ready", "xn_ready", "z_ready", "zmax_done", "z_used", "stat_saved"))
        xnT_mm, xnT_hi, xnT_lo = sem("xnT_mm"), sem("xnT_hi"), sem("xnT_lo")
        kT_mm, kT_hi, kT_lo, k_stacked = sem("kT_mm"), sem("kT_hi"), sem("kT_lo"), sem("k_stacked")
        q_mm, q_hi, q_lo, q_saved, q_loaded = sem("q_mm"), sem("q_hi"), sem("q_lo"), sem("q_saved"), sem("q_loaded")
        v_mm, v_ready = sem("v_mm"), sem("v_ready")
        kf_mm, kf_neg, kf_exp, kf_ready = sem("kf_mm"), sem("kf_neg"), sem("kf_exp"), sem("kf_ready")
        kf_hi, kf_hi_dve, kf_lo, v_hi = sem("kf_hi"), sem("kf_hi_dve"), sem("kf_lo"), sem("v_hi")
        kv_mm, kv_new_done, kv_hi, kv_saved = sem("kv_mm"), sem("kv_new_done"), sem("kv_hi"), sem("kv_saved")

        sp_held, pool_held, dve_held = sem("sp_held"), sem("pool_held"), sem("dve_held")
        zmT_in, scales_y = sem("zmT_in"), sem("scales_y")
        zm_part, zm_done, zmT_mm, zext_done, g_chain, zpart_mm, g_one, g_all, scales_ready = (
            sem(n) for n in ("zm_part", "zm_done", "zmT_mm", "zext_done", "g_chain", "zpart_mm", "g_one", "g_all", "scales_ready"))

        x2_loaded = [sem("x2_loaded0"), sem("x2_loaded1")]
        r_loaded = [sem("r_loaded0"), sem("r_loaded1")]
        stored = [sem("stored0"), sem("stored1")]
        stat_got, xnb_ready, zb_ready, res1_ready = (sem(n) for n in ("stat_got", "xnb_ready", "zb_ready", "res1_ready"))
        kv_ready = sem("kv_ready")
        qf_mm, qf_neg, qf_exp, qf_ready = sem("qf_mm"), sem("qf_neg"), sem("qf_exp"), sem("qf_ready")
        qf_hi, qf_lo_dve, qf_lo_pool = sem("qf_hi"), sem("qf_lo_dve"), sem("qf_lo_pool")
        h_lo_dve = sem("h_lo_dve")
        at_mm, den_done, rden_done, at_ready = sem("at_mm"), sem("den_done"), sem("rden_done"), sem("at_ready")
        at_hi, at_lo, aT_moved = sem("at_hi"), sem("at_lo"), sem("aT_moved")
        wo_mm, x1_sum, bn1_done, mv1_done, ve1_ready, rs1_ready, n1_ready = (
            sem(n) for n in ("wo_mm", "x1_sum", "bn1_done", "mv1_done", "ve1_ready", "rs1_ready", "n1_ready"))
        res2_part, res2_ready = sem("res2_part"), sem("res2_ready")
        n1_hi, n1_lo, nT_moved = sem("n1_hi"), sem("n1_lo"), sem("nT_moved")
        w1_mm, gelu_done, h_hi, h_lo, w2_mm = (sem(n) for n in ("w1_mm", "gelu_done", "h_hi", "h_lo", "w2_mm"))
        x2_sum, bn2_done, mv2_done, ve2_ready, rs2_ready, x2_scaled, out_ready = (
            sem(n) for n in ("x2_sum", "bn2_done", "mv2_done", "ve2_ready", "rs2_ready", "x2_scaled", "out_ready"))
        zT_mm, zq_affine, zq_clipped, zs_hi, zs_lo, y_mm, xb_ready, acc_ready = (
            sem(n) for n in ("zT_mm", "zq_affine", "zq_clipped", "zs_hi", "zs_lo", "y_mm", "xb_ready", "acc_ready"))

        def three_passes(pe, dst, weights, moving, chunks, first=True, last=True):
            steps = [(c, i, j) for c in chunks for i, j in PASSES]
            for n, (c, i, j) in enumerate(steps):
                mm = pe.matmul(dst, weights(c)[i], moving(c)[j], start=first and n == 0,
                               stop=last and n == len(steps) - 1)
            return mm

        def columns(parts, cols):
            return lambda c: tuple(p[:, c, cols] for p in parts)

        def tile_cols(t):
            return slice(t * P, (t + 1) * P)

        def group(b, u):
            return b * GPB + u

        def stat_cols(b, u):
            return stats[:, bass.ds(group(b, u) * 12, 12)]

        def kv_cols(b):
            return kv_all[:, bass.ds(b * (2 * KVW), 2 * KVW)]

        WEIGHT_SLOTS = (0, 1, 2, 3, 2, 3)

        def weight_blocks(n):
            if n < 2:
                raws = ((raw_qkv, 0), (raw_qkv, 2)) if n == 0 else ((raw_qkv, 4), (raw_out, 0))
                return [((2 * i + c) * D + r * P, raw[:, base + r, tile_cols(c)])
                        for i, (raw, base) in enumerate(raws) for c in range(KD) for r in range(2)]
            if n < 4:
                return [(r * P, raw_w1[:, r, tile_cols(n - 2)]) for r in range(FC)]
            return [(j * D + r * P, raw_w2[:, r, tile_cols(4 * (n - 4) + j)]) for j in range(4) for r in range(2)]

        def weight_parts(n, part):
            if n < 2:
                return [(w[part][:, :, :], ps[:, 2 * n + i, :].rearrange("p (k d) -> p k d", k=KD))
                        for i, w in enumerate(((wq, wk), (wv, wo))[n])]
            return [(w2s[part][:, 4 * (n - 4):4 * (n - 3), :].rearrange("p k d -> p (k d)"), pair_flat(WEIGHT_SLOTS[n]))]

        def by_chunks(rows):
            return rows.rearrange("p t (k d) -> p t k d", k=KD)

        def parts_by_tiles(part):
            return part.rearrange("p (k t d) -> p t k d", k=KD, t=TILES)

        def head_values(part, k, i):
            return vals[:, part, k, 2 * i:2 * i + 2].rearrange("p t (h e) -> p (t h) e", e=VW)[:, :, 0:HD]

        def stack_rows(eng, stack, rows, j, done):
            for r in range(P // PAIR_D):
                eng.dma_start(stack[j * PAIR_D:(j + 1) * PAIR_D, r::P // PAIR_D, :],
                              rows[r * PAIR_D:(r + 1) * PAIR_D, :, :]).then_inc(done, 16)

        block = ctx.enter_context(nc.Block())

        @block.sync
        def _(sp):
            def hold():
                sp.sem_inc(sp_held, 1)

            def load_a(b, u):
                if exists(b, u + 4):
                    if exists(b, u + 2):
                        sp.wait_ge(xnT_mm, nth(b, u + 2))
                        sp.wait_ge(z_ready, nth(b, u + 2))
                    sp.dma_start(xin[:, u % 2], x_rows[group(b, u + 4)]).then_inc(x_loaded[u % 2], 16)
                if exists(b, u + 2):
                    for part, places in ((0, (0, 2)), (1, (1,))):
                        sp.wait_ge((kT_hi, kT_lo)[part], nth(b, u + 2))
                        for j in places:
                            stack_rows(sp, k_stack[(u + 2) % 4], kT[:, part], j, k_stacked)
                    sp.wait_ge(q_lo, nth(b, u + 2, 2, 2))
                    for part in range(2):
                        sp.dma_start(q_parts[group(b, u + 2), part].rearrange("(m p) t -> p m t", p=P),
                                     qT[part][:]).then_inc(q_saved, 16)

            sp.dma_start(raw_qkv, w_qkv.rearrange("(r p) d -> p r d", p=P)).then_inc(ld_qkv, 16)
            load_a(0, -4)
            sp.dma_start(raw_out, w_out.rearrange("(r p) d -> p r d", p=P)).then_inc(ld_qkv, 16)
            sp.dma_start(raw_w1, w1.rearrange("(r p) d -> p r d", p=P)).then_inc(ld_w1, 16)
            sp.dma_start(raw_ffn, ffn_weight.rearrange("(k p) u -> p k u", p=P)).then_inc(ld_ffn, 16)
            sp.dma_start(raw_w2, w2.rearrange("(r p) f -> p r f", p=P)).then_inc(ld_w2, 16)
            for dst, src in ((gamma_col, gamma), (beta_col, beta), (lng_col, ln_gamma), (lnb_col, ln_beta), (b1_col, b1)):
                sp.dma_start(dst[:], src.rearrange("(k p) -> p k", p=P), allow_slow_non_contiguous=True).then_inc(ld_cols, 16)
            sp.wait_ge(proj_zero, 1)
            for j in range(len(PASSES)):
                for i in range(2):
                    row = j * PAIR_D + i * HD
                    sp.dma_start(raw_stack[row:row + HD, :, i * F:(i + 1) * F],
                                 proj.rearrange("(c i) d f -> i d c f", i=2)[i]).then_inc(ld_proj, 16)
            for dst, src in ((gamma_row, gamma), (beta_row, beta), (bout_row, b_out), (b2_row, b2)):
                sp.dma_start(dst[:], src.partition_broadcast(P)).then_inc(ld_rows, 16)
            over_groups(sp, load_a, 3)
            load_a(B - 1, GPB)
            sp.wait_ge(xnT_mm, GROUPS)
            sp.wait_ge(z_ready, GROUPS)
            sp.wait_ge(q_saved, 2 * 16 * GROUPS)

            def transpose_parts(b, u, parts, transposed, hi, lo, done):
                for part, ready in enumerate((hi, lo)):
                    sp.wait_ge(ready, nth(b, u))
                    hold()
                    sp.dma_start_transpose(transposed[part].rearrange("p k (t c) -> p (k t) c", c=P), parts[part][:]).then_inc(done, 16)

            def move_b(b, u):
                k = u % 2
                if exists(b, u + 2):
                    if exists(b, u):
                        sp.wait_ge(zT_mm, nth(b, u))
                    elif exists(b, u + 1):
                        sp.wait_ge(qf_mm, nth(b, u + 1, 4, 4))
                    for j, (_, part) in enumerate(PASSES):
                        sp.dma_start(q_stack[j * PAIR_D:(j + 1) * PAIR_D],
                                     q_parts[group(b, u + 2), part].rearrange("(c p) t -> p c t", p=PAIR_D)).then_inc(q_loaded, 16)
                if exists(b, u + 1):
                    transpose_parts(b, u + 1, at_parts, aT, at_hi, at_lo, aT_moved)
                if exists(b, u - 1):
                    sp.wait_ge(out_ready, nth(b, u - 1))
                    sp.dma_start(out_rows[group(b, u - 1)], xres[:, 1 - k]).then_inc(stored[1 - k], 16)
                if exists(b, u + 1):
                    if exists(b, u - 1):
                        sp.wait_ge(stored[1 - k], dma_nth(b, u - 1))
                    else:
                        sp.wait_ge(zm_done, 1)
                    sp.dma_start(xres[:, 1 - k], x_rows[group(b, u + 1)]).then_inc(r_loaded[1 - k], 16)
                if exists(b, u + 3):
                    if exists(b, u + 1):
                        sp.wait_ge(res1_ready, nth(b, u + 1))
                        sp.wait_ge(zb_ready, nth(b, u + 1))
                    sp.dma_start(xin[:, 1 - k], x_rows[group(b, u + 3)]).then_inc(x2_loaded[1 - k], 16)
                if exists(b, u + 1):
                    transpose_parts(b, u + 1, n1_parts, nT, n1_hi, n1_lo, nT_moved)

            over_groups(sp, move_b, 3)
            move_b(B - 1, GPB)
            for s in stored:
                sp.wait_ge(s, 16 * GROUPS // 2)

        @block.gpsimd
        def _(pool):
            def hold():
                pool.sem_inc(pool_held, 1)

            def flat(a):
                return a.rearrange("p t d -> p (t d)")

            def rows4(row):
                return row[:].unsqueeze(1).broadcast_to([P, TILES, D])

            pool.memset(ones[:], 1.0).then_inc(consts_set, 1)
            pool.memset(minus_half[:], -0.5).then_inc(consts_set, 1)
            pool.memset(ident[:], 0.0).then_inc(consts_set, 1)
            pool.wait_ge(consts_set, 3)
            pool.affine_select(out=ident[:], in_=ident[:], compare_op=ALU.not_equal, fill=1.0, base=0,
                               pattern=[[-1, P]], channel_multiplier=1).then_inc(consts_set, 1)
            pool.memset(zmax, -3.0e38).then_inc(zinit, 1)
            pool.memset(zmin, 3.0e38).then_inc(zinit, 1)
            pool.memset(vals[:, 0], 1.0).then_inc(vals_ones, 1)
            pool.memset(vals[:, 1], 0.0).then_inc(vals_ones, 1)

            def norm_a(b, u):
                k = (u + 3) % 2

                def low(w, t):
                    if exists(b, w):
                        if t == 3:
                            pool.wait_ge(kf_hi_dve, nth(b, w))
                        else:
                            pool.wait_ge(kf_hi, nth(b, w, t + 1, 3))
                        if exists(b, w - 1):
                            pool.wait_ge(kv_mm, nth(b, w - 1, t + 1, 4))
                        pool.tensor_tensor(key_fs[1][:, t, :], key_feat[t], key_fs[0][:, t, :], ALU.subtract).then_inc(kf_lo, 1)

                low(u - 1, 2)
                if exists(b, u + 3):
                    pool.wait_ge(pw_ready, nth(b, u + 3))
                    pool.tensor_tensor(stat[:, k, 0:8], pw[:], minus_half[:], ALU.pow).then_inc(std_ready, 1)
                low(u - 1, 3)
                low(u, 0)
                if exists(b, u + 3):
                    pool.wait_ge(std_ready, nth(b, u + 3))
                    hold()
                    for t in range(TILES):
                        last = pool.tensor_scalar(xin[:, k, t, :], xin[:, k, t, :], stat[:, k, 8 + t:9 + t],
                                                  stat[:, k, t:t + 1], ALU.add, ALU.mult)
                    last.then_inc(xn_ready, 1)
                    pool.wait_ge(xn_ready, nth(b, u + 3))
                    if exists(b, u + 2):
                        pool.wait_ge(z_used, nth(b, u + 2))
                    hold()
                    for t in range(TILES):
                        last = pool.tensor_scalar(z[:, t, :], xin[:, k, t, :], stat[:, k, 4 + t:5 + t], 1.0, ALU.mult, ALU.mult)
                    last.then_inc(z_ready, 1)
                low(u, 1)

            over_groups(pool, norm_a, 4)
            norm_a(B - 1, GPB)
            pool.wait_ge(z_used, GROUPS)
            pool.wait_ge(xnT_mm, GROUPS)

            def step_b(b, u):
                def hidden_low(p):
                    pool.wait_ge(h_hi, nth(b, u, p + 1, 4))
                    if exists(b, u - 1):
                        pool.wait_ge(w2_mm, nth(b, u - 1, 4, 4))
                    pool.tensor_tensor(flat(hid[1][:, 2 * p:2 * p + 2, :]), hidden[:, p % 2],
                                       flat(hid[0][:, 2 * p:2 * p + 2, :]).bitcast(F32), ALU.subtract).then_inc(h_lo, 1)

                if exists(b, u):
                    pool.wait_ge(zs_hi, nth(b, u))
                    pool.tensor_tensor(zs[1][:], zq, zs[0][:].bitcast(F32), ALU.subtract).then_inc(zs_lo, 1)
                    hidden_low(0)
                if exists(b, u - 1):
                    pool.wait_ge(ve2_ready, nth(b, u - 1))
                    pool.tensor_tensor(rs2[:], ve2[:], minus_half[:, 0:TILES], ALU.pow).then_inc(rs2_ready, 1)
                if exists(b, u):
                    hidden_low(1)
                    hidden_low(2)
                    pool.wait_ge(n1_ready, nth(b, u))
                    if exists(b, u - 1):
                        pool.wait_ge(x2_sum, nth(b, u - 1))
                    pool.tensor_tensor(res2[:], n1[:], rows4(gamma_row), ALU.mult).then_inc(res2_part, 1)
                    pool.wait_ge(res2_part, nth(b, u))
                    pool.tensor_tensor(res2[:], res2[:], rows4(b2_row), ALU.add).then_inc(res2_ready, 1)
                if exists(b, u + 1):
                    pool.wait_ge(ve1_ready, nth(b, u + 1))
                    pool.tensor_tensor(rs1[:], ve1[:], minus_half[:, 0:TILES], ALU.pow).then_inc(rs1_ready, 1)
                if exists(b, u + 2):
                    k = u % 2
                    pool.wait_ge(xnb_ready, nth(b, u + 2))
                    if exists(b, u + 1):
                        pool.wait_ge(x1_sum, nth(b, u + 1))
                    pool.tensor_tensor(res1[:], xin[:, k], rows4(bout_row), ALU.add).then_inc(res1_ready, 1)
                if exists(b, u + 1):
                    k = (u + 1) % 2
                    pool.wait_ge(r_loaded[k], dma_nth(b, u + 1))
                    pool.tensor_tensor(xres[:, k], xres[:, k], rows4(beta_row), ALU.add).then_inc(xb_ready, 1)
                if exists(b, u + 2):
                    for p in (0, 1):
                        pool.wait_ge(qf_hi, nth(b, u + 2, p + 1, 4))
                        pool.tensor_tensor(flat(query_fs[1][:, 2 * p:2 * p + 2, :]), query_feat[p],
                                           flat(query_fs[0][:, 2 * p:2 * p + 2, :]), ALU.subtract).then_inc(qf_lo_pool, 1)
                if exists(b, u + 3):
                    k = (u + 3) % 2
                    pool.wait_ge(x2_loaded[k], dma_nth(b, u + 3))
                    pool.wait_ge(stat_got, nth(b, u + 3))
                    hold()
                    for t in range(TILES):
                        last = pool.tensor_scalar(xin[:, k, t, :], xin[:, k, t, :], stat[:, k, 8 + t:9 + t],
                                                  stat[:, k, t:t + 1], ALU.add, ALU.mult)
                    last.then_inc(xnb_ready, 1)

            over_groups(pool, step_b, 3)
            step_b(B - 1, GPB)

        @block.scalar
        def _(act):
            def weight_high(n):
                act.wait_ge(wT_mm, n + 1)
                for hi, src in weight_parts(n, 0):
                    last = act.activation(hi, src, ACT.Copy, scale=W_SCALE if hi.dtype == F16 else 1.0)
                last.then_inc(wT_hi, 1)

            weight_high(0)
            weight_high(1)
            act.wait_ge(ld_ffn, 16)
            act.activation(tern_a, raw_ffn.rearrange("p k u -> p (k u)"), ACT.Abs, accum_out=colsum).then_inc(w_abs, 1)
            for n in (2, 3):
                act.wait_ge(wT_mm, n + 1)
                act.activation(w1T[:, n - 2, :], pair_flat(WEIGHT_SLOTS[n]), ACT.Copy, scale=W_SCALE).then_inc(w1_plain, 1)

            def other_parts():
                weight_high(4)
                weight_high(5)
                act.wait_ge(w1_plain, 2)
                act.wait_ge(ld_cols, 16 * 5)
                for c in range(KD):
                    last = act.activation(w1s[0][:, c, :], w1T[:, c, :], ACT.Copy, scale=gamma_col[:, c:c + 1])
                last.then_inc(wT_hi, 1)
                act.wait_ge(ld_proj, 6 * 16)
                act.copy(proj_stack[0:STACK], raw_stack[0:STACK]).then_inc(stack_hi, 1)

            def step_a(b, u, meanwhile=None):
                def high(w, t):
                    if exists(b, w):
                        act.wait_ge(kf_ready, nth(b, w, t + 1, 4))
                        if exists(b, w - 1):
                            act.wait_ge(kv_mm, nth(b, w - 1, t + 1, 4))
                        act.copy(key_fs[0][:, t, :], key_feat[t]).then_inc(kf_hi, 1)

                def values_high(i):
                    if exists(b, u + 1):
                        act.wait_ge(v_mm, nth(b, u + 1, i + 1, 2))
                        act.wait_ge(vals_ones, 2)
                        if exists(b, u - 1):
                            act.wait_ge(kv_mm, nth(b, u - 1, 2 * i + 2, 4))
                        act.copy(head_values(0, (u + 1) % 2, i), ps[:, 7, :].rearrange("p (h e) -> p h e", e=HD)).then_inc(v_hi, 1)

                def queries_high(i):
                    if exists(b, u + 2):
                        act.wait_ge(q_mm, nth(b, u + 2, i + 1, 2))
                        if exists(b, u + 1):
                            act.wait_ge(q_saved, nth(b, u + 1, 32, 32))
                        act.copy(qT[0][:, i, :], ps[:, (0, 7)[i], :]).then_inc(q_hi, 1)

                def negative_part(t):
                    if exists(b, u):
                        act.wait_ge(kf_mm, nth(b, u, t + 1, 4))
                        if exists(b, u - 1):
                            act.wait_ge(kf_lo, nth(b, u - 1, t + 1, 4))
                        act.activation(key_feat[t], pair_flat(1 + t % 2), ACT.Relu, scale=-1.0).then_inc(kf_neg, 1)

                def exponential(t):
                    if exists(b, u):
                        act.wait_ge(kf_neg, nth(b, u, t + 1, 4))
                        act.activation(key_feat[t], key_feat[t], ACT.Exp, scale=-1.0).then_inc(kf_exp, 1)

                negative_part(0)
                if exists(b, u + 2):
                    act.wait_ge(xnT_mm, nth(b, u + 2))
                    if exists(b, u):
                        act.wait_ge(v_mm, nth(b, u, 2, 2))
                    act.copy(xnTs[u % 2][0], pair(0)).then_inc(xnT_hi, 1)
                if meanwhile:
                    meanwhile()
                exponential(0)
                negative_part(1)
                values_high(0)
                exponential(1)
                high(u, 0)
                if exists(b, u + 2):
                    act.wait_ge(kT_mm, nth(b, u + 2))
                    if exists(b, u + 1):
                        act.wait_ge(k_stacked, nth(b, u + 1, 192, 192))
                    act.copy(kT[:, 0], pair(0)).then_inc(kT_hi, 1)
                negative_part(2)
                high(u, 1)
                values_high(1)
                exponential(2)
                negative_part(3)
                queries_high(0)
                exponential(3)
                high(u, 2)
                queries_high(1)

            step_a(0, -2, other_parts)
            over_groups(act, step_a, 1)
            step_a(B - 1, GPB)

            def step_b(b, u):
                def hidden_units(p):
                    act.wait_ge(w1_mm, nth(b, u, p + 1, 4))
                    if p >= 2:
                        act.wait_ge(h_lo, nth(b, u, p - 1, 3))
                    elif exists(b, u - 1):
                        if p == 0:
                            act.wait_ge(h_lo, nth(b, u - 1, 3, 3))
                        else:
                            act.wait_ge(h_lo_dve, nth(b, u - 1))
                    for a in range(2):
                        c = 2 * p + a
                        last = act.activation(hidden[:, p % 2, a * 512:(a + 1) * 512], ps[:, 2 * (p % 2) + a, :],
                                              ACT.Gelu, bias=b1_col[:, c:c + 1], scale=1.0 / W_SCALE)
                    last.then_inc(gelu_done, 1)
                    act.wait_ge(gelu_done, nth(b, u, p + 1, 4))
                    if exists(b, u - 1):
                        act.wait_ge(w2_mm, nth(b, u - 1, 4, 4))
                    act.copy(hid[0][:, 2 * p:2 * p + 2, :].rearrange("p a c -> p (a c)"), hidden[:, p % 2]).then_inc(h_hi, 1)

                def query_exp(p):
                    act.wait_ge(qf_mm, nth(b, u + 2, p + 1, 4))
                    if p == 0 and exists(b, u + 1):
                        act.wait_ge(at_lo, nth(b, u + 1))
                    elif p == 1 and exists(b, u - 1):
                        act.wait_ge(out_ready, nth(b, u - 1))
                    elif p == 2 and exists(b, u + 1):
                        act.wait_ge(qf_lo_dve, nth(b, u + 1, 1, 2))
                    elif p == 3 and exists(b, u + 1):
                        act.wait_ge(qf_lo_dve, nth(b, u + 1, 2, 2))
                    q = query_feat[p]
                    act.activation(q, pair_flat(QUERY_PAIRS[p]), ACT.Relu, scale=-1.0).then_inc(qf_neg, 1)
                    act.wait_ge(qf_neg, nth(b, u + 2, p + 1, 4))
                    act.activation(q, q, ACT.Exp, scale=-1.0).then_inc(qf_exp, 1)

                def query_high(p):
                    act.wait_ge(qf_ready, nth(b, u + 2, p + 1, 4))
                    if exists(b, u + 1):
                        act.wait_ge(at_mm, nth(b, u + 1, 2, 2))
                    act.copy(query_fs[0][:, 2 * p:2 * p + 2, :].rearrange("p a c -> p (a c)"), query_feat[p]).then_inc(qf_hi, 1)

                if exists(b, u):
                    hidden_units(0)
                if exists(b, u + 1):
                    act.wait_ge(at_ready, nth(b, u + 1, 2, 2))
                    if exists(b, u):
                        act.wait_ge(wo_mm, nth(b, u))
                    act.copy(parts_by_tiles(at_parts[0]), by_chunks(attn)).then_inc(at_hi, 1)
                if exists(b, u):
                    hidden_units(1)
                    hidden_units(2)
                if exists(b, u + 1):
                    k = (u + 1) % 2
                    act.wait_ge(xnb_ready, nth(b, u + 1))
                    if exists(b, u):
                        act.wait_ge(zs_lo, nth(b, u))
                    for t in range(TILES):
                        last = act.activation(z[:, t, :], xin[:, k, t, :], ACT.Copy, scale=stat[:, k, 4 + t:5 + t])
                    last.then_inc(zb_ready, 1)
                if exists(b, u):
                    hidden_units(3)
                if exists(b, u + 2):
                    query_exp(0)
                    query_exp(1)
                    query_exp(2)
                    query_high(0)
                if exists(b, u + 1):
                    act.wait_ge(n1_ready, nth(b, u + 1))
                    if exists(b, u):
                        act.wait_ge(w1_mm, nth(b, u, 4, 4))
                    act.copy(parts_by_tiles(n1_parts[0]), by_chunks(n1)).then_inc(n1_hi, 1)
                if exists(b, u + 2):
                    query_exp(3)
                    query_high(1)
                    query_high(2)
                    query_high(3)
                if exists(b, u + 1):
                    act.wait_ge(zT_mm, nth(b, u + 1))
                    act.wait_ge(scales_ready, 1)
                    if exists(b, u):
                        act.wait_ge(zs_lo, nth(b, u))
                    for c in range(KD):
                        last = act.activation(zq[:, c, :], ps[:, 6 + c, :], ACT.Identity, bias=bz[:, c:c + 1], scale=gz[:, c:c + 1])
                    last.then_inc(zq_affine, 1)

            over_groups(act, step_b, 3)
            step_b(B - 1, GPB)

        @block.vector
        def _(dve):
            def hold():
                dve.sem_inc(dve_held, 1)

            dve.memset(x2[:], 0.0).then_inc(proj_zero, 1)
            dve.memset(kv_mask[:], 0.0).then_inc(mask_zero, 1)
            dve.wait_ge(mask_zero, 1)
            mask_c = kv_mask[:].rearrange("p (c w) -> p c w", w=CW)
            dve.memset(mask_c[0:F, :, 0:VW], KV_SCALE).then_inc(mask_ready, 1)
            dve.memset(mask_c[F:P, :, VW:CW], KV_SCALE).then_inc(mask_ready, 1)

            def low_parts(n, done):
                dve.wait_ge(wT_hi, done)
                for (lo, src), (hi, _) in zip(weight_parts(n, 1), weight_parts(n, 0)):
                    if hi.dtype == F16:
                        last = dve.scalar_tensor_tensor(lo, src, W_SCALE, hi, ALU.mult, ALU.subtract)
                    else:
                        last = dve.tensor_tensor(lo, src, hi.bitcast(F32), ALU.subtract)
                last.then_inc(wT_lo, 1)

            def second_weights():
                low_parts(4, 3)
                low_parts(5, 4)
                step_a(0, -3)

            def other_parts():
                dve.wait_ge(wT_hi, 5)
                for c in range(KD):
                    last = dve.scalar_tensor_tensor(w1s[1][:, c, :], w1T[:, c, :], gamma_col[:, c:c + 1],
                                                    w1s[0][:, c, :], ALU.mult, ALU.subtract)
                last.then_inc(wT_lo, 1)
                dve.wait_ge(stack_hi, 1)
                low_rows = slice(STACK - PAIR_D, STACK)
                dve.tensor_tensor(proj_stack[low_rows], raw_stack[low_rows], proj_stack[low_rows], ALU.subtract).then_inc(stack_lo, 1)

            def other_weights():
                dve.wait_ge(b1_mm, 1)
                dve.wait_ge(ld_cols, 16 * 5)
                dve.scalar_tensor_tensor(b1_col[:], ps[:, 2, 0:FC], 1.0 / W_SCALE, b1_col[:], ALU.mult, ALU.add).then_inc(b1_done, 1)
                dve.wait_ge(ld_rows, 16 * 4)
                dve.tensor_tensor(b2_row[:], b2_row[:], beta_row[:], ALU.add).then_inc(w_chain, 1)
                dve.wait_ge(w_sum, 1)
                dve.tensor_scalar(w_mean, ps[:, 3, 0:1], 1.0 / (D * D), None, ALU.mult).then_inc(w_chain, 1)
                dve.wait_ge(w_chain, 2)
                dve.tensor_scalar(w_half, w_mean, EPS_FFN, 0.5, ALU.add, ALU.mult).then_inc(w_chain, 1)
                dve.tensor_scalar(y_scale, w_mean, 1.0 / QB, None, ALU.mult).then_inc(w_chain, 1)
                dve.wait_ge(w_chain, 3)
                dve.tensor_scalar(w_minus_half, w_half, -1.0, None, ALU.mult).then_inc(w_chain, 1)
                flat_ffn = raw_ffn.rearrange("p k u -> p (k u)")
                dve.tensor_scalar(tern_a, flat_ffn, w_half, None, ALU.is_gt).then_inc(w_chain, 1)
                dve.wait_ge(w_chain, 6)
                dve.tensor_scalar(tern_b, flat_ffn, w_minus_half, None, ALU.is_lt).then_inc(w_chain, 1)
                dve.wait_ge(w_chain, 7)
                dve.tensor_tensor(ternary[:].rearrange("p k u -> p (k u)"), tern_a, tern_b, ALU.subtract).then_inc(tern_done, 1)

            def moments(b, u, src, bn_t, mv_t, bn_s, mv_s):
                for t in range(TILES):
                    last = dve.bn_stats(bn_t[:, t, :], src[:, t, :])
                last.then_inc(bn_s, 1)
                dve.wait_ge(bn_s, nth(b, u))
                hold()
                for t in range(TILES):
                    last = dve.bn_aggr(mv_t[:, t, :], bn_t[:, t, :])
                last.then_inc(mv_s, 1)
                dve.wait_ge(mv_s, nth(b, u))

            def step_a(b, u, meanwhile=None, later=None):
                def extremes(best, op, done):
                    if exists(b, u + 2):
                        dve.wait_ge(z_ready, nth(b, u + 2))
                        if exists(b, u + 1):
                            dve.wait_ge(done, nth(b, u + 1))
                        else:
                            dve.wait_ge(zinit, 2)
                        dve.tensor_tensor(best, best, z[:], op).then_inc(done, 1)

                def feature_sum(t):
                    if exists(b, u):
                        dve.wait_ge(kf_exp, nth(b, u, t + 1, 4))
                        dve.scalar_tensor_tensor(key_feat[t], pair_flat(1 + t % 2), 0.0, key_feat[t],
                                                 ALU.max, ALU.add).then_inc(kf_ready, 1)

                def values_low(i):
                    if exists(b, u + 1):
                        k = (u + 1) % 2
                        dve.wait_ge(v_hi, nth(b, u + 1, i + 1, 2))
                        dve.tensor_tensor(head_values(1, k, i), ps[:, 7, :].rearrange("p (h e) -> p h e", e=HD), head_values(0, k, i),
                                          ALU.subtract).then_inc(v_ready, 1)

                def queries_low(i):
                    if exists(b, u + 2):
                        dve.wait_ge(q_hi, nth(b, u + 2, i + 1, 2))
                        dve.tensor_tensor(qT[1][:, i, :], ps[:, (0, 7)[i], :], qT[0][:, i, :], ALU.subtract).then_inc(q_lo, 1)

                ahead = exists(b, u + 4)
                k = u % 2
                if exists(b, u + 2):
                    dve.wait_ge(xnT_hi, nth(b, u + 2))
                    dve.tensor_tensor(xnTs[k][1], pair(0), xnTs[k][0].bitcast(F32), ALU.subtract).then_inc(xnT_lo, 1)
                feature_sum(0)
                values_low(0)
                extremes(zmax, ALU.max, zmax_done)
                if meanwhile:
                    meanwhile()
                feature_sum(1)
                if exists(b, u + 2):
                    dve.wait_ge(kT_hi, nth(b, u + 2))
                    dve.tensor_tensor(kT[:, 1], pair(0), kT[:, 0], ALU.subtract).then_inc(kT_lo, 1)
                    dve.tensor_copy(stat_cols(b, u + 2), stat[:, k, :]).then_inc(stat_saved, 1)
                extremes(zmin, ALU.min, z_used)
                values_low(1)
                if later:
                    later()
                batch_ends = u % GPB == 0 and exists(b, u - 1)
                if batch_ends:
                    dve.wait_ge(kv_mm, nth(b, u - 1, 4, 4))
                    dve.wait_ge(mask_ready, 2)
                    dve.tensor_tensor(kv_new, ps[:, 6, 0:KVW], kv_mask[:], ALU.mult).then_inc(kv_new_done, 1)
                if ahead:
                    dve.wait_ge(x_loaded[k], dma_nth(b, u + 4))
                    for t in range(TILES):
                        last = dve.bn_stats(bn[:, t, :], xin[:, k, t, :])
                    last.then_inc(bn_done, 1)
                feature_sum(2)
                if ahead:
                    dve.wait_ge(bn_done, nth(b, u + 4))
                    hold()
                    for t in range(TILES):
                        last = dve.bn_aggr(mv[:, t, :], bn[:, t, :])
                    last.then_inc(mv_done, 1)
                if batch_ends:
                    saved = kv_cols(b + u // GPB - 1)
                    dve.wait_ge(kv_new_done, b + u // GPB)
                    dve.tensor_copy(saved[:, 0:KVW], kv_new).then_inc(kv_hi, 1)
                queries_low(0)
                if ahead:
                    dve.wait_ge(mv_done, nth(b, u + 4))
                    if exists(b, u + 2):
                        dve.wait_ge(stat_saved, nth(b, u + 2))
                    dve.tensor_scalar(stat[:, k, 8:12], mv[:, :, 0], -1.0, None, ALU.mult)
                    if exists(b, u + 3):
                        dve.wait_ge(std_ready, nth(b, u + 3))
                    dve.tensor_scalar(pw[:, 0:TILES], mv[:, :, 1], EPS_LN, None, ALU.add).then_inc(ve_done, 1)
                if ahead:
                    dve.wait_ge(ve_done, nth(b, u + 4))
                    dve.reciprocal(inv[:], pw[:, 0:TILES]).then_inc(inv_done, 1)
                if batch_ends:
                    dve.wait_ge(kv_hi, b + u // GPB)
                    dve.tensor_tensor(saved[:, KVW:2 * KVW], kv_new, saved[:, 0:KVW], ALU.subtract).then_inc(kv_saved, 1)
                feature_sum(3)
                if ahead:
                    dve.wait_ge(inv_done, nth(b, u + 4))
                    dve.tensor_tensor(inv[:], inv[:], mv[:, :, 1], ALU.mult).then_inc(ratio_done, 1)
                queries_low(1)
                if ahead:
                    dve.wait_ge(ratio_done, nth(b, u + 4))
                    dve.tensor_scalar(pw[:, TILES:8], inv[:], EPS_FFN_LN, None, ALU.add).then_inc(pw_ready, 1)
                if exists(b, u):
                    dve.wait_ge(kf_ready, nth(b, u, 4, 4))
                    if exists(b, u - 1):
                        dve.wait_ge(kv_mm, nth(b, u - 1, 4, 4))
                    dve.tensor_copy(key_fs[0][:, 3, :], key_feat[3]).then_inc(kf_hi_dve, 1)

            step_a(0, -4)
            low_parts(0, 1)
            low_parts(1, 2)
            step_a(0, -2, second_weights, other_parts)
            step_a(0, -1, other_weights)
            over_groups(dve, step_a, 0, GPB - 2)
            dve.wait_ge(zmax_done, GROUPS)
            dve.wait_ge(z_used, GROUPS)
            zf = [zmax.rearrange("p t d -> p (t d)"), zmin.rearrange("p t d -> p (t d)")]
            for step, width in enumerate((2 * D, D)):
                for a, op in zip(zf, (ALU.max, ALU.min)):
                    last = dve.tensor_tensor(a[:, 0:width], a[:, 0:width], a[:, width:2 * width], op)
                    last.then_inc(zm_part if step == 0 else zmT_in, 1)
                dve.wait_ge(zm_part, 2)
            step_a(B - 1, GPB - 2)
            dve.wait_ge(zmT_mm, 1)
            dve.tensor_reduce(zext[:, 0:2], ps[:, 0, 0:256].rearrange("p (k n) -> p k n", k=2), AX_X, ALU.max)
            dve.tensor_reduce(zext[:, 2:4], ps[:, 0, 256:512].rearrange("p (k n) -> p k n", k=2), AX_X, ALU.min).then_inc(zext_done, 1)
            dve.wait_ge(zext_done, 1)
            for i in range(2):
                last = dve.tensor_tensor(zext[:, 2 * i:2 * i + 2], zext[:, 2 * i:2 * i + 2], lng_col[:], ALU.mult)
            last.then_inc(g_chain, 1)
            dve.wait_ge(g_chain, 1)
            for i in range(2):
                last = dve.tensor_tensor(zext[:, 2 * i:2 * i + 2], zext[:, 2 * i:2 * i + 2], lnb_col[:], ALU.add)
            last.then_inc(g_chain, 1)
            dve.wait_ge(g_chain, 2)
            dve.tensor_scalar(zabs, zext, -1.0, None, ALU.mult).then_inc(g_chain, 1)
            dve.wait_ge(g_chain, 3)
            dve.tensor_tensor(zabs, zabs, zext, ALU.max).then_inc(g_chain, 1)
            dve.wait_ge(g_chain, 4)
            dve.tensor_reduce(zpart, zabs, AX_X, ALU.max).then_inc(zm_done, 1)
            step_a(B - 1, GPB - 1)
            dve.wait_ge(zpart_mm, 1)
            dve.tensor_reduce(small[0:1, 21:22], ps[0:1, 7, 0:P], AX_X, ALU.max).then_inc(g_one, 1)
            step_a(B - 1, GPB)
            dve.wait_ge(g_all, 1)
            dve.tensor_copy(gmax, ps[:, 7, P:P + 1]).then_inc(g_chain, 1)
            dve.wait_ge(g_chain, 5)
            dve.reciprocal(qscale, gmax).then_inc(g_chain, 1)
            dve.tensor_tensor(y_scale, y_scale, gmax, ALU.mult).then_inc(scales_y, 1)
            dve.wait_ge(g_chain, 6)
            dve.tensor_scalar(gz, lng_col[:], qscale, QB, ALU.mult, ALU.mult)
            dve.tensor_scalar(bz, lnb_col[:], qscale, QB, ALU.mult, ALU.mult).then_inc(scales_ready, 1)

            def flat(a):
                return a.rearrange("p t d -> p (t d)")

            def step_b(b, u):
                def query_sum(p):
                    dve.wait_ge(qf_exp, nth(b, u + 2, p + 1, 4))
                    dve.scalar_tensor_tensor(query_feat[p], pair_flat(QUERY_PAIRS[p]), 0.0, query_feat[p],
                                             ALU.max, ALU.add).then_inc(qf_ready, 1)

                def query_low(p):
                    dve.wait_ge(qf_hi, nth(b, u + 2, p + 1, 4))
                    dve.tensor_tensor(flat(query_fs[1][:, 2 * p:2 * p + 2, :]), query_feat[p],
                                      flat(query_fs[0][:, 2 * p:2 * p + 2, :]), ALU.subtract).then_inc(qf_lo_dve, 1)

                if exists(b, u + 1):
                    for n, a in enumerate((1, 0)):
                        dve.wait_ge(at_mm, nth(b, u + 1, n + 1, 2))
                        sums = ps[:, 4 + 2 * a:6 + 2 * a, 0:KVW].rearrange("p t (h e) -> p t h e", e=VW)
                        r = rden[:, 2 * a:2 * a + 2, :]
                        dve.tensor_scalar(r, sums[:, :, :, HD], EPS_ATTN * KV_SCALE, None, ALU.add).then_inc(den_done, 1)
                        dve.wait_ge(den_done, nth(b, u + 1, n + 1, 2))
                        dve.reciprocal(r, r).then_inc(rden_done, 1)
                        dve.wait_ge(rden_done, nth(b, u + 1, n + 1, 2))
                        dve.tensor_tensor(attn[:, 2 * a:2 * a + 2, :].rearrange("p t (h e) -> p t h e", e=HD),
                                          sums[:, :, :, 0:HD], r.unsqueeze(3).broadcast_to([P, 2, H, HD]),
                                          ALU.mult).then_inc(at_ready, 1)
                if exists(b, u - 1):
                    dve.wait_ge(x2_sum, nth(b, u - 1))
                    moments(b, u - 1, x2, bn2, mv2, bn2_done, mv2_done)
                    if exists(b, u - 2):
                        dve.wait_ge(rs2_ready, nth(b, u - 2))
                    dve.tensor_scalar(ve2[:], mv2[:, :, 1], EPS_LN, None, ALU.add).then_inc(ve2_ready, 1)
                if exists(b, u + 1):
                    dve.wait_ge(at_hi, nth(b, u + 1))
                    dve.tensor_tensor(parts_by_tiles(at_parts[1]), by_chunks(attn), parts_by_tiles(at_parts[0]),
                                      ALU.subtract).then_inc(at_lo, 1)
                if exists(b, u - 1):
                    k = (u - 1) % 2
                    for t in range(TILES):
                        last = dve.scalar_tensor_tensor(x2[:, t, :], x2[:, t, :], mv2[:, t, 0:1], gamma_row[:],
                                                        ALU.subtract, ALU.mult)
                    last.then_inc(x2_scaled, 1)
                    dve.wait_ge(x2_scaled, nth(b, u - 1))
                    dve.wait_ge(rs2_ready, nth(b, u - 1))
                    dve.wait_ge(acc_ready, nth(b, u - 1))
                    for t in range(TILES):
                        last = dve.scalar_tensor_tensor(xres[:, k, t, :], x2[:, t, :], rs2[:, t:t + 1], xres[:, k, t, :],
                                                        ALU.mult, ALU.add)
                    last.then_inc(out_ready, 1)
                if exists(b, u):
                    k = u % 2
                    dve.wait_ge(y_mm, nth(b, u))
                    dve.wait_ge(xb_ready, nth(b, u))
                    dve.scalar_tensor_tensor(flat(xres[:, k]), pair_flat(0), y_scale, flat(xres[:, k]),
                                             ALU.mult, ALU.add).then_inc(acc_ready, 1)
                if exists(b, u):
                    dve.wait_ge(h_hi, nth(b, u, 4, 4))
                    dve.tensor_tensor(flat(hid[1][:, 6:8, :]), hidden[:, 1], flat(hid[0][:, 6:8, :]).bitcast(F32),
                                      ALU.subtract).then_inc(h_lo_dve, 1)
                if exists(b, u + 1):
                    dve.wait_ge(wo_mm, nth(b, u + 1))
                    dve.wait_ge(res1_ready, nth(b, u + 1))
                    if exists(b, u):
                        dve.wait_ge(res2_part, nth(b, u))
                    dve.scalar_tensor_tensor(flat(n1), pair_flat(3), 1.0 / W_SCALE, flat(res1), ALU.mult, ALU.add).then_inc(x1_sum, 1)
                if exists(b, u + 1):
                    dve.wait_ge(x1_sum, nth(b, u + 1))
                    for t in range(TILES):
                        last = dve.bn_stats(bn1[:, t, :], n1[:, t, :])
                    last.then_inc(bn1_done, 1)
                    dve.wait_ge(bn1_done, nth(b, u + 1))
                    hold()
                    for t in range(TILES):
                        last = dve.bn_aggr(mv1[:, t, :], bn1[:, t, :])
                    last.then_inc(mv1_done, 1)
                    dve.wait_ge(mv1_done, nth(b, u + 1))
                    if exists(b, u):
                        dve.wait_ge(rs1_ready, nth(b, u))
                    dve.tensor_scalar(ve1[:], mv1[:, :, 1], EPS_LN, None, ALU.add).then_inc(ve1_ready, 1)
                if exists(b, u + 2):
                    query_sum(0)
                if exists(b, u + 1):
                    dve.wait_ge(rs1_ready, nth(b, u + 1))
                    hold()
                    for t in range(TILES):
                        last = dve.tensor_scalar(n1[:, t, :], n1[:, t, :], mv1[:, t, 0:1], rs1[:, t:t + 1], ALU.subtract, ALU.mult)
                    last.then_inc(n1_ready, 1)
                if exists(b, u + 2):
                    query_sum(1)
                if exists(b, u + 1):
                    dve.wait_ge(n1_hi, nth(b, u + 1))
                    dve.tensor_tensor(parts_by_tiles(n1_parts[1]), by_chunks(n1), parts_by_tiles(n1_parts[0]),
                                      ALU.subtract).then_inc(n1_lo, 1)
                if exists(b, u + 2):
                    query_sum(2)
                    query_sum(3)
                    query_low(2)
                    query_low(3)
                    if (u + 2) % GPB == 0:
                        dve.wait_ge(kv_saved, B)
                        if exists(b, u + 1):
                            dve.wait_ge(at_mm, nth(b, u + 1, 2, 2))
                        dve.tensor_copy(kv_cur, kv_cols(b + (u + 2) // GPB)).then_inc(kv_ready, 1)
                if exists(b, u + 3):
                    k = (u + 3) % 2
                    if exists(b, u + 1):
                        dve.wait_ge(zb_ready, nth(b, u + 1))
                    dve.tensor_copy(stat[:, k, :], stat_cols(b, u + 3)).then_inc(stat_got, 1)
                if exists(b, u):
                    dve.wait_ge(w2_mm, nth(b, u, 4, 4))
                    dve.wait_ge(res2_ready, nth(b, u))
                    if exists(b, u - 1):
                        dve.wait_ge(out_ready, nth(b, u - 1))
                    if exists(b, u + 2):
                        dve.wait_ge(qf_lo_pool, nth(b, u + 2, 2, 2))
                    dve.tensor_tensor(flat(x2), pair_flat(1), flat(res2), ALU.add).then_inc(x2_sum, 1)
                if exists(b, u + 1):
                    dve.wait_ge(zq_affine, nth(b, u + 1))
                    dve.tensor_scalar(zq, zq, CLIP, -CLIP, ALU.min, ALU.max).then_inc(zq_clipped, 1)
                    dve.wait_ge(zq_clipped, nth(b, u + 1))
                    if exists(b, u):
                        dve.wait_ge(y_mm, nth(b, u))
                    dve.tensor_copy(zs[0][:], zq).then_inc(zs_hi, 1)

            over_groups(dve, step_b, 3)
            step_b(B - 1, GPB)

        @block.tensor
        def _(pe):
            pe.wait_ge(consts_set, 4)

            def transposed_weights(n):
                for col, src in weight_blocks(n):
                    last = pe.transpose(pair_flat(WEIGHT_SLOTS[n])[:, col:col + P], src, ident[:])
                last.then_inc(wT_mm, 1)

            pe.wait_ge(ld_qkv, 32)
            transposed_weights(0)
            transposed_weights(1)
            pe.wait_ge(ld_w1, 16)
            transposed_weights(2)
            transposed_weights(3)

            def second_weights():
                pe.wait_ge(ld_w2, 16)
                for n in (4, 5):
                    pe.wait_ge(w1_plain, n - 3)
                    transposed_weights(n)

            def other_sums():
                pe.wait_ge(w1_plain, 2)
                pe.wait_ge(ld_cols, 16 * 5)
                for c in range(FC):
                    for d in range(KD):
                        last = pe.matmul(ps[:, 2, c:c + 1], w1T[:, d, c * P:(c + 1) * P], beta_col[:, d:d + 1],
                                         start=(c == 0 and d == 0), stop=(c == FC - 1 and d == KD - 1), skip_group_check=True)
                last.then_inc(b1_mm, 1)
                pe.wait_ge(w_abs, 1)
                pe.matmul(ps[:, 3, 0:1], ones[:], colsum, start=True, stop=True).then_inc(w_sum, 1)
                pe.wait_ge(wT_lo, 4)

            pe.wait_ge(wT_lo, 2)

            def transposes(dst, src):
                for c in range(KD):
                    for t in range(TILES):
                        last = pe.transpose(dst[:, c, tile_cols(t)], src[:, t, tile_cols(c)], ident[:])
                return last

            def query_features(b, u, p):
                if not exists(b, u + 2):
                    return
                if p == 0:
                    pe.wait_ge(q_loaded, nth(b, u + 2, 48, 48))
                    if exists(b, u + 1):
                        pe.wait_ge(at_ready, nth(b, u + 1, 2, 2))
                elif p == 1:
                    if exists(b, u):
                        pe.wait_ge(acc_ready, nth(b, u))
                    elif exists(b, u + 1):
                        pe.wait_ge(qf_ready, nth(b, u + 1, 2, 4))
                elif p == 2:
                    if exists(b, u + 1):
                        pe.wait_ge(x1_sum, nth(b, u + 1))
                    else:
                        pe.wait_ge(kv_new_done, B)
                        pe.wait_ge(g_chain, 5)
                else:
                    pe.wait_ge(qf_ready, nth(b, u + 2, 1, 4))
                for a in range(2):
                    c = 2 * p + a
                    last = pe.matmul(ps[:, 2 * QUERY_PAIRS[p] + a, :], proj_stack[0:STACK, c, :], q_stack[0:STACK, c, :],
                                     start=True, stop=True)
                last.then_inc(qf_mm, 1)

            def step_a(b, u, meanwhile=None, later=None):
                def key_features(t):
                    if not exists(b, u):
                        return
                    if t == 0:
                        pe.wait_ge(k_stacked, nth(b, u, 192, 192))
                    if t >= 2:
                        pe.wait_ge(kf_ready, nth(b, u, t - 1, 4))
                    elif exists(b, u - 1):
                        pe.wait_ge(kf_ready, nth(b, u - 1, t + 3, 4))
                    for c in range(HC):
                        last = pe.matmul(pair_flat(1 + t % 2)[:, c * P:(c + 1) * P], k_stack[u % 4][0:STACK, c, tile_cols(t)],
                                         proj_stack[0:STACK, c, :], start=True, stop=True)
                    last.then_inc(kf_mm, 1)

                def values(i):
                    if not exists(b, u + 1):
                        return
                    pe.wait_ge(xnT_lo, nth(b, u + 1))
                    if i == 1:
                        pe.wait_ge(v_ready, nth(b, u + 1, 1, 2))
                    else:
                        pe.wait_ge(q_lo, nth(b, u + 1, 2, 2))
                    rows = xnTs[(u + 1) % 2]
                    for t in range(2):
                        last = three_passes(pe, ps[:, 7, t * D:(t + 1) * D], columns(rows, tile_cols(2 * i + t)),
                                            columns(wv, slice(None)), range(KD))
                    last.then_inc(v_mm, 1)

                def queries(i):
                    if not exists(b, u + 2):
                        return
                    if i == 0:
                        pe.wait_ge(kT_lo, nth(b, u + 2))
                    elif exists(b, u + 1):
                        pe.wait_ge(v_ready, nth(b, u + 1, 2, 2))
                    three_passes(pe, ps[:, (0, 7)[i], :], columns(wq, tile_cols(i)), columns(xnTs[u % 2], slice(None)),
                                 range(KD)).then_inc(q_mm, 1)

                def sums(w, i):
                    if not exists(b, w):
                        return
                    pe.wait_ge(kf_lo, nth(b, w, i + 1, 4))
                    if i % 2 == 0:
                        pe.wait_ge(v_ready, nth(b, w, i // 2 + 1, 2))
                    if i == 0 and w % GPB == 0 and exists(b, w - 1):
                        pe.wait_ge(kv_new_done, b + w // GPB)
                    for c in range(HC):
                        first = w % GPB == 0 and i == 0 and c == 0
                        end = w % GPB == GPB - 1 and i == TILES - 1 and c == HC - 1
                        for n, (f, v) in enumerate(PASSES):
                            last = pe.matmul(ps[:, 6, c * CW:(c + 1) * CW], key_fs[f][:, i, c * P:(c + 1) * P],
                                             vals[:, v, w % 2, i, c * CW:(c + 1) * CW], start=first and n == 0,
                                             stop=end and n == len(PASSES) - 1, skip_group_check=True)
                    last.then_inc(kv_mm, 1)

                key_features(0)
                if exists(b, u + 2):
                    pe.wait_ge(xn_ready, nth(b, u + 2))
                    if exists(b, u + 1):
                        pe.wait_ge(q_lo, nth(b, u + 1, 1, 2))
                    transposes(pair(0), xin[:, u % 2]).then_inc(xnT_mm, 1)
                if meanwhile:
                    meanwhile()
                sums(u - 1, 1)
                key_features(1)
                values(0)
                sums(u - 1, 2)
                if exists(b, u + 2):
                    pe.wait_ge(xnT_lo, nth(b, u + 2))
                    for m in range(KD):
                        last = three_passes(pe, ps[:, m, :], columns(wk, tile_cols(m)), columns(xnTs[u % 2], slice(None)), range(KD))
                    last.then_inc(kT_mm, 1)
                if later:
                    later()
                key_features(2)
                values(1)
                sums(u - 1, 3)
                queries(0)
                key_features(3)
                sums(u, 0)
                queries(1)

            step_a(0, -2, second_weights, other_sums)
            step_a(0, -1)
            pe.wait_ge(stack_lo, 1)
            pe.wait_ge(b1_done, 1)
            pe.wait_ge(w_chain, 2)
            over_groups(pe, step_a, 0, GPB - 1)
            pe.wait_ge(zmT_in, 2)
            pe.wait_ge(q_lo, 2 * GROUPS)
            for n, a in enumerate((zmax, zmin)):
                for c in range(KD):
                    col = (n * KD + c) * P
                    last = pe.transpose(ps[:, 0, col:col + P], a.rearrange("p t d -> p (t d)")[:, c * P:(c + 1) * P], ident[:])
            last.then_inc(zmT_mm, 1)
            step_a(B - 1, GPB - 1)
            pe.wait_ge(zm_done, 1)
            pe.wait_ge(v_ready, 2 * GROUPS)
            pe.transpose(ps[0:1, 7, 0:P], zpart, ident[:]).then_inc(zpart_mm, 1)
            pe.wait_ge(kf_ready, TILES * GROUPS)
            query_features(0, -2, 0)
            query_features(0, -2, 1)
            step_a(B - 1, GPB)
            pe.wait_ge(g_one, 1)
            pe.matmul(ps[:, 7, P:P + 1], ones[0:1, :], small[0:1, 21:22], start=True, stop=True).then_inc(g_all, 1)

            def step_b(b, u):
                def hidden_units(p):
                    if p == 0:
                        pe.wait_ge(nT_moved, nth(b, u, 32, 32))
                        if exists(b, u + 1):
                            pe.wait_ge(qf_ready, nth(b, u + 1, 2, 4))
                        else:
                            pe.wait_ge(acc_ready, nth(b, u - 1))
                    elif p == 1:
                        if exists(b, u - 1):
                            pe.wait_ge(x2_sum, nth(b, u - 1))
                    else:
                        pe.wait_ge(gelu_done, nth(b, u, p - 1, 4))
                    for a in range(2):
                        c = 2 * p + a
                        last = three_passes(pe, ps[:, 2 * (p % 2) + a, :], columns(w1s, tile_cols(c)),
                                            columns(nT, slice(None)), range(KD))
                    last.then_inc(w1_mm, 1)

                def out_tile(t):
                    if not exists(b, u):
                        return
                    if t == 0:
                        pe.wait_ge(gelu_done, nth(b, u, 4, 4))
                        pe.wait_ge(h_lo, nth(b, u, 3, 3))
                    for part in range(2):
                        if t == 0 and part == 1:
                            pe.wait_ge(h_lo_dve, nth(b, u))
                        last = three_passes(pe, pair_flat(1)[:, t * D:(t + 1) * D], columns(hid, tile_cols(t)),
                                            columns(w2s, slice(None)), (range(FC - 2), range(FC - 2, FC))[part],
                                            first=part == 0, last=part == 1)
                    last.then_inc(w2_mm, 1)

                if exists(b, u):
                    hidden_units(0)
                if exists(b, u + 1):
                    pe.wait_ge(qf_hi, nth(b, u + 1, 4, 4))
                    pe.wait_ge(qf_lo_dve, nth(b, u + 1, 2, 2))
                    pe.wait_ge(qf_lo_pool, nth(b, u + 1, 2, 2))
                    pe.wait_ge(kv_ready, b + (u + 1) // GPB + 1)
                    if exists(b, u):
                        pe.wait_ge(zq_affine, nth(b, u))
                    for t in (2, 3, 0, 1):
                        for c in range(HC):
                            for n, (f, v) in enumerate(PASSES):
                                last = pe.matmul(ps[:, 4 + t, c * CW:(c + 1) * CW], query_fs[f][:, c, tile_cols(t)],
                                                 kv_cur[:, v * KVW + c * CW:v * KVW + (c + 1) * CW], start=(c == 0 and n == 0),
                                                 stop=(c == HC - 1 and n == len(PASSES) - 1), skip_group_check=True)
                        if t % 2:
                            last.then_inc(at_mm, 1)
                if exists(b, u):
                    hidden_units(1)
                    hidden_units(2)
                    hidden_units(3)
                if u > -2:
                    query_features(b, u, 0)
                if exists(b, u):
                    pe.wait_ge(zs_lo, nth(b, u))
                    pe.wait_ge(gelu_done, nth(b, u, 3, 4))
                    for t in range(TILES):
                        steps = [(c, part) for c in range(KD) for part in zs]
                        for n, (c, part) in enumerate(steps):
                            last = pe.matmul(pair_flat(0)[:, t * D:(t + 1) * D], part[:, c, tile_cols(t)], ternary[:, c, :],
                                             start=(n == 0), stop=(n == len(steps) - 1))
                    last.then_inc(y_mm, 1)
                if exists(b, u + 1):
                    pe.wait_ge(aT_moved, nth(b, u + 1, 32, 32))
                    for t in range(TILES):
                        last = three_passes(pe, pair_flat(3)[:, t * D:(t + 1) * D], columns(aT, tile_cols(t)),
                                            columns(wo, slice(None)), range(KD))
                    last.then_inc(wo_mm, 1)
                if u > -2:
                    query_features(b, u, 1)
                out_tile(0)
                query_features(b, u, 2)
                out_tile(1)
                query_features(b, u, 3)
                out_tile(2)
                out_tile(3)
                if exists(b, u + 1):
                    pe.wait_ge(zb_ready, nth(b, u + 1))
                    if exists(b, u + 2):
                        pe.wait_ge(qf_ready, nth(b, u + 2, 3, 4))
                    else:
                        pe.wait_ge(x1_sum, nth(b, u + 1))
                    transposes(pair(3), z).then_inc(zT_mm, 1)

            pe.wait_ge(kv_saved, B)
            pe.wait_ge(wT_lo, 5)
            pe.wait_ge(tern_done, 1)
            over_groups(pe, step_b, 3)
            step_b(B - 1, GPB)


_INS = ['L0_attn_x', 'L0_attn_proj', 'L0_attn_w_qkv', 'L0_attn_w_out', 'L0_attn_b_out', 'L0_attn_gamma', 'L0_attn_beta',
        'L0_attn_w1', 'L0_attn_b1', 'L0_attn_w2', 'L0_attn_b2', 'L0_ffn_weight', 'L0_ffn_ln_gamma', 'L0_ffn_ln_beta']
_OUTS = [((B, N, D), 'float32')]


def kernel(**inputs):
    import numpy as _np
    import concourse.bacc as _bacc
    from concourse import mybir as _mybir
    from concourse.bass_utils import run_bass_kernel_spmd as _run

    nc = _bacc.Bacc("TRN2", target_bir_lowering=False, num_devices=1)
    arrays, args = {}, []
    for name in _INS:
        a = _np.ascontiguousarray(inputs[name])
        arrays[f"in_{name}_dram"] = a
        args.append(nc.dram_tensor(f"in_{name}_dram", a.shape, _mybir.dt.from_np(a.dtype), kind="ExternalInput").ap())
    for i, (shape, dtype) in enumerate(_OUTS):
        dt = _mybir.dt.from_np(_np.dtype(dtype))
        args.append(nc.dram_tensor(f"out_{i}_dram", shape, dt, kind="ExternalOutput").ap())
    linear_attention_block(nc, *args)
    r = _run(nc, [arrays], core_ids=[0])
    got = tuple(r.results[0][f"out_{i}_dram"] for i in range(len(_OUTS)))
    return got[0]
```
